# Optimizing a Trainium2 kernel written in Bass

```python
import numpy as np
import jax
import jax.numpy as jnp

def _softmax(x, axis=-1):
    return jax.nn.softmax(x, axis=axis)

def _gelu(x):
    return jax.nn.gelu(x, approximate=True)

def _silu(x):
    return jax.nn.silu(x)

def _sigmoid(x):
    return jax.nn.sigmoid(x)

def _layernorm(x, axis=-1, eps=1e-05):
    m = jnp.mean(x, axis=axis, keepdims=True)
    v = jnp.var(x, axis=axis, keepdims=True)
    return (x - m) / jnp.sqrt(v + eps)

def _scatter_add(tgt, idx, src, axis=0):
    return tgt.at[idx].add(src)

def _segment_sum(src, seg, n):
    return jax.ops.segment_sum(src, seg, n)
kernel_name = 'mk_seq_postln_d1_jaxref_r8_ee2948'

def setup_inputs(seed: int=0):
    np.random.seed(seed)
    _w = jnp.asarray

    def _L0_attn_setup():
        import jax, jax.numpy as jnp
        import numpy as np
        D_MODEL = 128
        N_HEADS = 16
        SEQ_LEN = 256
        BATCH = 4
        D_HEAD = D_MODEL // N_HEADS
        key = jax.random.key(seed)
        ks = jax.random.split(key, 5)
        s = 1.0 / np.sqrt(D_MODEL)
        x = jax.random.normal(ks[0], (BATCH, SEQ_LEN, D_MODEL), dtype=jnp.float32)
        W_qkv = jax.random.uniform(ks[1], (3 * D_MODEL, D_MODEL), jnp.float32, -s, s)
        b_qkv = jax.random.uniform(ks[2], (3 * D_MODEL,), jnp.float32, -s, s)
        W_o = jax.random.uniform(ks[3], (D_MODEL, D_MODEL), jnp.float32, -s, s)
        b_o = jax.random.uniform(ks[4], (D_MODEL,), jnp.float32, -s, s)
        return {'x': x, 'W_qkv': W_qkv, 'b_qkv': b_qkv, 'W_o': W_o, 'b_o': b_o}
    _L0_attn_in = _L0_attn_setup()

    def _L0_ffn_setup():
        import jax, jax.numpy as jnp
        import numpy as np
        B, T, D = (2, 256, 128)
        DCD = 512
        RET = 128
        NEXP = 512
        NKEYS = 64
        H = 4
        KPH = 8
        key = jax.random.key(seed)
        ks = jax.random.split(key, 10)
        s = lambda k, shape, scale: jax.random.normal(k, shape, jnp.float32) * scale
        return {'hidden_states': jax.random.normal(ks[0], (B, T, D), jnp.float32), 'Wg': s(ks[1], (D, DCD), 0.02), 'bg': jnp.zeros((DCD,), jnp.float32), 'Wu': s(ks[2], (D, DCD), 0.02), 'bu': jnp.zeros((DCD,), jnp.float32), 'Wd': s(ks[3], (DCD, D), 0.02), 'bd': jnp.zeros((D,), jnp.float32), 'Wq': s(ks[4], (D, RET * H), 0.02), 'keys': s(ks[5], (H, NKEYS, 2, RET // 2), 0.02), 'down_embed': s(ks[6], (NEXP, D), 0.02), 'up_embed': s(ks[7], (NEXP, D), 0.02)}
    _L0_ffn_in = _L0_ffn_setup()
    _d = {'L0_attn_x': _L0_attn_in['x'], 'L0_attn_W_qkv': _L0_attn_in['W_qkv'], 'L0_attn_b_qkv': _L0_attn_in['b_qkv'], 'L0_attn_W_o': _L0_attn_in['W_o'], 'L0_attn_b_o': _L0_attn_in['b_o'], 'L0_ffn_Wg': _L0_ffn_in['Wg'], 'L0_ffn_bg': _L0_ffn_in['bg'], 'L0_ffn_Wu': _L0_ffn_in['Wu'], 'L0_ffn_bu': _L0_ffn_in['bu'], 'L0_ffn_Wd': _L0_ffn_in['Wd'], 'L0_ffn_bd': _L0_ffn_in['bd'], 'L0_ffn_Wq': _L0_ffn_in['Wq'], 'L0_ffn_keys': _L0_ffn_in['keys'], 'L0_ffn_down_embed': _L0_ffn_in['down_embed'], 'L0_ffn_up_embed': _L0_ffn_in['up_embed']}
    _x0 = _d['L0_attn_x']
    _d['L0_attn_x'] = jax.random.normal(jax.random.fold_in(jax.random.key(seed), 1), (4, 1024, 128), dtype=_x0.dtype)
    del _x0
    return _d

def reference(L0_attn_x, L0_attn_W_qkv, L0_attn_b_qkv, L0_attn_W_o, L0_attn_b_o, L0_ffn_Wg, L0_ffn_bg, L0_ffn_Wu, L0_ffn_bu, L0_ffn_Wd, L0_ffn_bd, L0_ffn_Wq, L0_ffn_keys, L0_ffn_down_embed, L0_ffn_up_embed):

    def _L0_attn_ref(x, W_qkv, b_qkv, W_o, b_o):
        import jax, jax.numpy as jnp
        import numpy as np
        D_MODEL = 128
        N_HEADS = 16
        SEQ_LEN = 256
        BATCH = 4
        D_HEAD = D_MODEL // N_HEADS
        b, t, d = x.shape
        qkv = x @ W_qkv.T + b_qkv
        qkv = qkv.reshape(b, t, 3, N_HEADS, D_HEAD)
        Q, K, V = jnp.moveaxis(qkv, 2, 0)
        Q = Q.transpose(0, 2, 1, 3)
        K = K.transpose(0, 2, 1, 3)
        V = V.transpose(0, 2, 1, 3)
        scores = jnp.einsum('bhqd,bhkd->bhqk', Q, K) / np.sqrt(D_HEAD)
        causal = jnp.triu(jnp.full((t, t), -jnp.inf, dtype=scores.dtype), k=1)
        attn = jax.nn.softmax(scores + causal, axis=-1)
        O = jnp.einsum('bhqk,bhkd->bhqd', attn, V)
        O = O.transpose(0, 2, 1, 3).reshape(b, t, d)
        return O @ W_o.T + b_o

    def _L0_ffn_ref(hidden_states, Wg, bg, Wu, bu, Wd, bd, Wq, keys, down_embed, up_embed):
        import jax, jax.numpy as jnp
        import numpy as np
        B, T, D = (2, 256, 128)
        DCD = 512
        RET = 128
        NEXP = 512
        NKEYS = 64
        H = 4
        KPH = 8
        b, t, d = hidden_states.shape
        q = (hidden_states @ Wq).reshape(b, t, 2, H, RET // 2)
        sim = jnp.einsum('btphn,hkpn->pbthk', q, keys)
        sc, ix = jax.lax.top_k(sim, KPH)
        sx, sy = (sc[0], sc[1])
        ixx, ixy = (ix[0], ix[1])
        all_sc = (sx[..., :, None] + sy[..., None, :]).reshape(b, t, H, KPH * KPH)
        all_ix = (ixx[..., :, None] * NKEYS + ixy[..., None, :]).reshape(b, t, H, KPH * KPH)
        scores, pk = jax.lax.top_k(all_sc, KPH)
        idx = jnp.take_along_axis(all_ix, pk, axis=-1)
        de = down_embed[idx]
        ue = up_embed[idx]
        w = jnp.einsum('btd,bthkd->bthk', hidden_states, de)
        w = jax.nn.silu(w) * jax.nn.softmax(scores, axis=-1)
        experts_states = jnp.einsum('bthk,bthkd->btd', w, ue)
        mlp = jax.nn.silu(hidden_states @ Wg + bg) * (hidden_states @ Wu + bu) @ Wd + bd
        return mlp + experts_states
    x = L0_attn_x
    x = _layernorm(x + _L0_attn_ref(x, L0_attn_W_qkv, L0_attn_b_qkv, L0_attn_W_o, L0_attn_b_o), axis=-1)
    x = _layernorm(x + _L0_ffn_ref(x, L0_ffn_Wg, L0_ffn_bg, L0_ffn_Wu, L0_ffn_bu, L0_ffn_Wd, L0_ffn_bd, L0_ffn_Wq, L0_ffn_keys, L0_ffn_down_embed, L0_ffn_up_embed), axis=-1)
    return x

_drawn_inputs = setup_inputs


def setup_inputs(seed=0):
    import zlib

    import numpy as np

    out = dict(_drawn_inputs(seed))
    spreads = {'L0_ffn_bg': (0.0, 0.8), 'L0_ffn_bu': (0.0, 0.8), 'L0_ffn_bd': (0.0, 0.1)}
    factors = {'L0_ffn_Wg': 4.416,
     'L0_ffn_Wu': 4.35,
     'L0_ffn_Wd': 3.949,
     'L0_ffn_Wq': 8.0,
     'L0_ffn_keys': 8.0,
     'L0_ffn_down_embed': 7.049,
     'L0_ffn_up_embed': 7.42}
    for name, (base, spread) in spreads.items():
        noise = np.random.default_rng([zlib.crc32(name.encode()), seed]).standard_normal(out[name].shape)
        drawn = base * np.exp(spread * noise) if base else spread * noise
        out[name] = jnp.asarray(drawn.astype(out[name].dtype))
    for name, factor in factors.items():
        out[name] = (out[name] * factor).astype(out[name].dtype)
    return out
```

```python
from contextlib import ExitStack

import concourse.bass as bass
from concourse import mybir

F32 = mybir.dt.float32
BF16 = mybir.dt.bfloat16
U32 = mybir.dt.uint32
ALU = mybir.AluOpType
ACT = mybir.ActivationFunctionType
AX = mybir.AxisListType

P = 128
BATCH, SEQ, D = 4, 1024, 128
HEADS, DH = 16, 8
TOKENS = BATCH * SEQ
TILES = TOKENS // P
CHUNK = 512
CHUNKS = TOKENS // CHUNK
TPC = CHUNK // P
HG = 4
GH = HEADS // HG
GROUPS = BATCH * HG
PARTS = 3
SPLIT_ROWS = PARTS * PARTS * DH
M_ROW = SPLIT_ROWS
VW = DH + 1
F = 512
FC = F // P
NEXP = 512
NK = 64
RH = 4
KPH = 8
XIN = NEXP // NK
EPS = 1e-5
SM_SCALE = float(DH) ** -0.5
BIG = 3.0e38
MARKED = 2.9e38
FAR = 1.0e38

UNITS = []
for _half, _tiles in ((0, (0, 1)), (0, (2, 3)), (1, (0, 1)), (1, (2, 3)), (1, (4, 5)), (1, (6, 7))):
    _at, _off = [], 0
    for _j in _tiles:
        _q0 = max(P * _j, CHUNK * _half)
        _w = CHUNK * (_half + 1) - _q0
        _at.append((_j, _q0, _w, _off))
        _off += _w
    UNITS.append((_half, _at, _off))
NU = len(UNITS)
DIAG_UNITS = [k for k, (h, at, w) in enumerate(UNITS) if at[0][0] >= 4 * h]
SPG = NU * GH
MPG = len(DIAG_UNITS) * GH

MAXC = []
for _i in range(SEQ // P - 1, -1, -1):
    _end = P * (_i + 1)
    for _part, (_c0, _c1) in enumerate([(0, CHUNK), (CHUNK, _end)] if _end > CHUNK else [(0, _end)]):
        for _hh in range(GH):
            MAXC.append((_i, _part, _hh, _c0, _c1))
CPG = len(MAXC)
AHEAD = 16
X_SLOTS = 3
FREE = 2
ONE = 1
S_BANK, O_BANK, X_BANK = 0, 4, 5
M_STEPS = 6
LINKS = 60


def wait_alone(eng, signal, value, done):
    if not isinstance(value, int):
        value = eng.to_reg(value)
    eng.wait_ge(done, 1)
    eng.wait_ge(signal, value)


def interleave():
    order, ta, td, e, f = [], 0.0, 0.0, 0, 0
    while e < SPG or f < CPG:
        if f >= CPG or (e < SPG and ta <= td):
            order.append(("s", e))
            ta += UNITS[e // GH][2] * 0.83 + 120
            e += 1
        else:
            order.append(("x", f))
            i, part, hh, c0, c1 = MAXC[(f + AHEAD) % CPG]
            td += (c1 - c0) * 1.04 + 80
            f += 1
    return order


def build(nc, x, W_qkv, b_qkv, W_o, b_o, Wg, bg, Wu, bu, Wd, bd, Wq, keys, down, up, out):
    order = interleave()
    q_scr = nc.dram_tensor("q_scr", [GROUPS, GH, 5, DH, SEQ], BF16).ap()
    k_scr = nc.dram_tensor("k_scr", [GROUPS, GH, PARTS, DH, SEQ], BF16).ap()
    m_scr = nc.dram_tensor("m_scr", [GROUPS, P, PARTS * 32], BF16).ap()
    o_scr = nc.dram_tensor("o_scr", [GROUPS, P, SEQ], F32).ap()

    with ExitStack() as ctx:
        def sb(name, shape, dt=F32):
            return ctx.enter_context(nc.sbuf_tensor(name, shape, dt))

        def sem(name):
            return ctx.enter_context(nc.semaphore(name))

        ps = ctx.enter_context(nc.psum_tensor("ps", [P, 8, 512], F32))

        ident = sb("ident", [P, P])
        WqkvT = sb("WqkvT", [P, 3, P])
        WoT = sb("WoT", [P, P])
        downT = sb("downT", [P, NEXP])
        Wsim = sb("Wsim", [P, 4, P])
        Wg_sb = sb("Wg_sb", [P, F])
        Wu_sb = sb("Wu_sb", [P, F])
        Wd_sb = sb("Wd_sb", [P, FC, D])
        up_sb = sb("up_sb", [P, FC, D])
        bqk = sb("bqk", [P, 2])
        bgu = sb("bgu", [P, 2, FC])
        bv_row = sb("bv_row", [P, D])
        bo_row = sb("bo_row", [P, D])
        bd_row = sb("bd_row", [P, D])
        iota8 = sb("iota8", [P, XIN])
        mhalf = sb("mhalf", [P, TPC])

        x_loaded = [sem(f"x_loaded{u}") for u in range(2)]
        wqkv_loaded = sem("wqkv_loaded")
        prep_loaded = sem("prep_loaded")
        wts_loaded = sem("wts_loaded")
        kbd_zeroed = sem("kbd_zeroed")
        consts_made = sem("consts_made")
        wT_ready = sem("wT_ready")
        wT_read = sem("wT_read")
        xT_ready = sem("xT_ready")
        xT_read = sem("xT_read")
        qk_ready = sem("qk_ready")
        v_ready = sem("v_ready")
        q_read = sem("q_read")
        v_read = sem("v_read")
        r_made = sem("r_made")
        p2_made = sem("p2_made")
        p3_made = sem("p3_made")
        qk_stored = [sem(f"qk_stored{u}") for u in range(2)]
        pads_made = sem("pads_made")
        xop_loaded = [sem(f"xop_loaded{u}") for u in range(2)]
        sop_loaded = [sem(f"sop_loaded{u}") for u in range(2)]
        mrow_loaded = [sem(f"mrow_loaded{u}") for u in range(2)]
        mx_ready = sem("mx_ready")
        mx_read = sem("mx_read")
        m_chain = sem("m_chain")
        m_stored = sem("m_stored")
        v_staged = sem("v_staged")
        s_ready = sem("s_ready")
        exp_done = sem("exp_done")
        masked = sem("masked")
        pv_done = sem("pv_done")
        o_read = sem("o_read")
        o_stored = [sem(f"o_stored{h}") for h in range(2)]
        ot_loaded = sem("ot_loaded")
        oT_ready = sem("oT_ready")
        attn_ready = sem("attn_ready")
        attnT_ready = sem("attnT_ready")
        attnT_copied = sem("attnT_copied")
        y_ready = sem("y_ready")
        xb_ready = sem("xb_ready")
        z_done = sem("z_done")
        var_ready = sem("var_ready")
        rstd_ready = sem("rstd_ready")
        x1_ready = sem("x1_ready")
        x1T_ready = sem("x1T_ready")
        x1T_copied = sem("x1T_copied")
        ffn_ready = sem("ffn_ready")
        ffn_read = sem("ffn_read")
        h_ready = sem("h_ready")
        sim_ready = sem("sim_ready")
        sim_copied = sem("sim_copied")
        route_done = sem("route_done")
        cand_ready = sem("cand_ready")
        shifted = sem("shifted")
        exps_ready = sem("exps_ready")
        edge_ready = sem("edge_ready")
        de_ready = sem("de_ready")
        A_ready = sem("A_ready")
        AT_ready = sem("AT_ready")
        Wt_ready = sem("Wt_ready")
        out_ready = sem("out_ready")
        x1b_ready = sem("x1b_ready")
        z2_done = sem("z2_done")
        var2_ready = sem("var2_ready")
        rstd2_ready = sem("rstd2_ready")
        fin_ready = sem("fin_ready")
        out_stored = sem("out_stored")
        c_chain = sem("c_chain")
        mv_done = sem("mv_done")
        xc_loaded = sem("xc_loaded")

        x_chunks = x.rearrange("b (h t p) d -> (b h) p t d", h=SEQ // CHUNK, p=P)
        out_chunks = out.rearrange("b (h t p) d -> (b h) p t d", h=SEQ // CHUNK, p=P)
        vaug = sb("vaug", [P, GROUPS, SEQ // P, GH, VW])

        with ExitStack() as phase:
            def sa(name, shape, dt=F32):
                return phase.enter_context(nc.sbuf_tensor(name, shape, dt))

            wqkv_nat = sa("wqkv_nat", [P, 3, P])
            wo_nat = sa("wo_nat", [P, P])
            down_nat = sa("down_nat", [P, FC, D])
            wq_nat = sa("wq_nat", [P, F])
            kbdT = sa("kbdT", [P, 4, P])
            WqT = sa("WqT", [P, 4, P])
            kbd = sa("kbd", [P, 4, P])
            xin = sa("xin", [P, 2, TPC, D])
            xT = sa("xT", [P, 2, CHUNK])
            qf = sa("qf", [P, 2, 2, CHUNK])
            rf = sa("rf", [P, 2, 2, CHUNK])
            qs = sa("qs", [P, 2, 2, PARTS, CHUNK], BF16)

            with nc.Block() as block:
                @block.sync
                def _(sp):
                    for signal in (*qk_stored, v_ready, p3_made, s_ready, *o_stored, o_read, oT_ready, xb_ready, z_done,
                                   out_ready, h_ready, Wt_ready, sim_copied, attn_ready, out_stored):
                        sp.sem_inc(signal, ONE)
                    sp.dma_start(down_nat[:], down.rearrange("(c p) d -> p c d", p=P)).then_inc(prep_loaded, 16)
                    sp.dma_start(wq_nat[:], Wq).then_inc(prep_loaded, 16)
                    sp.dma_start(wo_nat[:], W_o).then_inc(prep_loaded, 16)
                    sp.wait_ge(kbd_zeroed, 1)
                    for p in range(2):
                        for h in range(RH):
                            hl = h % 2
                            sp.dma_start(kbdT[64 * hl:64 * hl + 64, 2 * p + h // 2, 64 * hl:64 * hl + 64],
                                         keys[h, :, p, :]).then_inc(prep_loaded, 16)
                    sp.dma_start(Wg_sb[:], Wg).then_inc(wts_loaded, 16)
                    sp.dma_start(Wu_sb[:], Wu).then_inc(wts_loaded, 16)
                    sp.dma_start(Wd_sb[:], Wd.rearrange("(c p) d -> p c d", p=P)).then_inc(wts_loaded, 16)
                    sp.dma_start(up_sb[:], up.rearrange("(c p) d -> p c d", p=P)).then_inc(wts_loaded, 16)
                    for i, bias in enumerate((bg, bu)):
                        sp.dma_start(bgu[:, i, :], bias.rearrange("(c p) -> p c", p=P),
                                     allow_slow_non_contiguous=True).then_inc(wts_loaded, 16)
                    sp.dma_start(bo_row[:], b_o.rearrange("(o d) -> o d", o=1).broadcast_to([P, D])).then_inc(wts_loaded, 16)
                    sp.dma_start(bd_row[:], bd.rearrange("(o d) -> o d", o=1).broadcast_to([P, D])).then_inc(wts_loaded, 16)
                    with sp.Fori(0, BATCH) as b:
                        for u in range(2):
                            sp.wait_ge(p3_made, 4 * b + 2 * u + 2 + ONE)
                            for s in range(5):
                                dst = q_scr[bass.ds(b * HG, HG), :, s, :, CHUNK * u:CHUNK * (u + 1)]
                                sp.dma_start(dst.rearrange("n h d t -> (n h) d t"),
                                             qs[:, u, 0, s % PARTS, :]).then_inc(qk_stored[u], 16)
                            for s in range(PARTS):
                                dst = k_scr[bass.ds(b * HG, HG), :, s, :, CHUNK * u:CHUNK * (u + 1)]
                                sp.dma_start(dst.rearrange("n h d t -> (n h) d t"),
                                             qs[:, u, 1, s, :]).then_inc(qk_stored[u], 16)
                    for u in range(2):
                        sp.wait_ge(qk_stored[u], 128 * BATCH + ONE)
                    sp.wait_ge(wts_loaded, 16 * 8)

                @block.gpsimd
                def _(pool):
                    pool.memset(ident[:], 0.0).then_inc(consts_made, 1)
                    pool.wait_ge(consts_made, 1)
                    pool.affine_select(out=ident[:], in_=ident[:], compare_op=ALU.not_equal, fill=1.0, base=0,
                                       pattern=[[1, P]], channel_multiplier=-1).then_inc(consts_made, 1)
                    pool.memset(kbdT[:], 0.0).then_inc(kbd_zeroed, 1)
                    pool.memset(vaug[:], 1.0).then_inc(consts_made, 1)
                    pool.memset(mhalf[:], -0.5)
                    pool.iota(iota8[:], pattern=[[1, XIN]], base=0, channel_multiplier=0,
                              allow_small_or_imprecise_dtypes=True).then_inc(consts_made, 1)

                    with pool.Fori(0, BATCH) as b:
                        for u in range(2):
                            for w in range(2):
                                pool.wait_ge(p2_made, 4 * b + 2 * u + w + 1)
                                pool.tensor_tensor(qs[:, u, w, 2, :], rf[:, u, w, :], qs[:, u, w, 1, :],
                                                   ALU.subtract).then_inc(p3_made, 1)

                @block.scalar
                def _(act):
                    act.dma_start(wqkv_nat[:], W_qkv.rearrange("(c p) d -> p c d", p=P)).then_inc(wqkv_loaded, 16)
                    bqkv = b_qkv.rearrange("(w p) -> p w", w=3)
                    act.dma_start(bqk[:], bqkv[:, 0:2], allow_slow_non_contiguous=True).then_inc(wqkv_loaded, 16)
                    act.dma_start(bv_row[:], b_qkv.rearrange("(w d) -> w d", w=3)[2:3, :].broadcast_to([P, D])).then_inc(wqkv_loaded, 16)
                    for u in range(2):
                        act.dma_start(xin[:, u, :, :], x_chunks[u]).then_inc(x_loaded[u], 16)
                    for n, (bank, dst) in enumerate(((0, WqkvT[:, :, :]), (1, WoT[:, :]), (2, downT[:, :]),
                                                     (3, WqT[:, :, :]), (4, kbd[:, :, :]), (5, Wsim[:, :, :]))):
                        act.wait_ge(wT_ready, n + 1)
                        src = ps[:, bank, 0:dst.free_size()]
                        if len(dst.shape) == 3:
                            src = src.rearrange("p (a b) -> p a b", b=P)
                        act.activation(dst, src, ACT.Copy).then_inc(wT_read, 1)
                    act.wait_ge(wqkv_loaded, 48)
                    act.sem_inc(q_read, 2 * FREE)

                    def first_parts(b, more):
                        for u in range(2):
                            if more:
                                act.wait_ge(xT_ready, 2 * b + u + 1)
                                act.dma_start(xin[:, u, :, :], x_chunks[bass.ds(2 * b + u + 2, 1)].rearrange(
                                    "c p t d -> (c p) t d")).then_inc(x_loaded[u], 16)
                            act.wait_ge(qk_stored[u], 128 * b + ONE)
                            for w in range(2):
                                act.wait_ge(qk_ready, 4 * b + 2 * u + w + 1)
                                act.activation(qf[:, u, w, :], ps[:, 2 + 2 * w + u, :], ACT.Identity,
                                               bias=bqk[:, w:w + 1])
                                act.activation(qs[:, u, w, 0, :], ps[:, 2 + 2 * w + u, :], ACT.Identity,
                                               bias=bqk[:, w:w + 1]).then_inc(q_read, 1)

                    with act.Fori(0, BATCH - 1) as b:
                        first_parts(b, True)
                    first_parts(BATCH - 1, False)

                @block.tensor
                def _(pe):
                    pe.wait_ge(consts_made, 2)
                    pe.wait_ge(wqkv_loaded, 48)
                    for w in range(3):
                        mm = pe.transpose(ps[:, 0, P * w:P * (w + 1)], wqkv_nat[:, w, :], ident[:])
                    mm.then_inc(wT_ready, 1)
                    pe.wait_ge(prep_loaded, 16 * 11)
                    pe.transpose(ps[:, 1, 0:P], wo_nat[:], ident[:]).then_inc(wT_ready, 1)
                    for bank, blocks in ((2, [down_nat[:, c, :] for c in range(4)]),
                                         (3, [wq_nat[:, P * c:P * (c + 1)] for c in range(4)]),
                                         (4, [kbdT[:, c, :] for c in range(4)])):
                        for c in range(4):
                            mm = pe.transpose(ps[:, bank, P * c:P * (c + 1)], blocks[c], ident[:])
                        mm.then_inc(wT_ready, 1)
                    pe.wait_ge(wT_read, 5)
                    for c in range(4):
                        mm = pe.matmul(ps[:, 5, P * c:P * (c + 1)], WqT[:, c, :], kbd[:, c, :], start=True, stop=True)
                    mm.then_inc(wT_ready, 1)
                    pe.wait_ge(wT_read, 6)
                    with pe.Fori(0, BATCH) as b:
                        for u in range(2):
                            n = 2 * b + u
                            pe.wait_ge(x_loaded[u], 16 * b + 16)
                            pe.wait_ge(xT_read, n + 1)
                            for t in range(TPC):
                                mm = pe.transpose(ps[:, u, P * t:P * (t + 1)], xin[:, u, t, :], ident[:])
                            mm.then_inc(xT_ready, 1)
                            pe.wait_ge(xT_read, n + 1 + FREE)
                            for w in range(2):
                                pe.wait_ge(q_read, 2 * n + w + 1)
                                pe.matmul(ps[:, 2 + 2 * w + u, :], WqkvT[:, w, :], xT[:, u, :],
                                          start=True, stop=True).then_inc(qk_ready, 1)
                            pe.wait_ge(v_read, n + 1)
                            for t in range(TPC):
                                mm = pe.matmul(ps[:, 6 + u, P * t:P * (t + 1)], xT[:, u, P * t:P * (t + 1)],
                                               WqkvT[:, 2, :], start=True, stop=True)
                            mm.then_inc(v_ready, 1)

                @block.vector
                def _(dve):
                    dve.sem_inc(xT_read, FREE)
                    dve.sem_inc(v_read, FREE)
                    dve.wait_ge(consts_made, 3)
                    dve.wait_ge(wqkv_loaded, 48)
                    with dve.Fori(0, BATCH) as b:
                        for u in range(2):
                            n = 2 * b + u
                            dve.wait_ge(xT_ready, n + 1)
                            dve.wait_ge(v_ready, 2 * b + ONE)
                            dve.tensor_copy(xT[:, u, :], ps[:, u, :]).then_inc(xT_read, 1)
                            for w in range(2):
                                dve.wait_ge(q_read, 2 * n + w + 1 + 2 * FREE)
                                dve.wait_ge(p3_made, 4 * b + ONE)
                                dve.tensor_tensor(rf[:, u, w, :], qf[:, u, w, :], qs[:, u, w, 0, :],
                                                  ALU.subtract).then_inc(r_made, 1)
                                dve.wait_ge(r_made, 2 * n + w + 1)
                                dve.tensor_copy(qs[:, u, w, 1, :], rf[:, u, w, :]).then_inc(p2_made, 1)
                            dve.wait_ge(v_ready, n + 1 + ONE)
                            for t in range(TPC):
                                dst = vaug[:, bass.ds(b * HG, HG), TPC * u + t, :, 0:DH]
                                dd = dve.tensor_tensor(dst, ps[:, 6 + u, P * t:P * (t + 1)].rearrange(
                                    "p (g h d) -> p g h d", g=HG, d=DH), bv_row[:].rearrange(
                                    "p (g h d) -> p g h d", g=HG, d=DH), ALU.add)
                            dd.then_inc(v_read, 1)

        with ExitStack() as phase:
            def sa(name, shape, dt=F32):
                return phase.enter_context(nc.sbuf_tensor(name, shape, dt))

            Qx = sa("Qx", [P, 2, GH, SEQ], BF16)
            Kx = sa("Kx", [P, 2, GH, SEQ], BF16)
            Qa = sa("Qa", [P, 2, GH, SEQ], BF16)
            Ka = sa("Ka", [P, 2, GH, SEQ], BF16)
            probs = sa("probs", [P, 2, GH, 2 * CHUNK])
            Vg = sa("Vg", [P, 2, SEQ // P, GH, VW])
            Os = sa("Os", [P, 2, CHUNK])
            tri = sa("tri", [P, CHUNK])
            junk = sa("junk", [P, 4, CHUNK], BF16)
            mx = sa("mx", [P, GH, SEQ // P, 2])
            mm_ = sa("rowmax", [P, 32])
            mr = sa("mr", [P, 32])
            msp = sa("msp", [P, PARTS * 32], BF16)
            mT = sa("mT", [P, PARTS * 32], BF16)

            with nc.Block() as block:
                @block.sync
                def _(sp):
                    def load_parts(qdst, kdst, g, done):
                        rows = PARTS * DH
                        for r in range(PARTS):
                            src = q_scr[g, :, r:r + PARTS, :, :].rearrange("n h s d t -> (n s d) h t")
                            sp.dma_start(qdst[rows * r:rows * (r + 1), :, :], src).then_inc(done, 16)
                            sp.dma_start(kdst[rows * r:rows * (r + 1), :, :],
                                         k_scr[g].rearrange("n h s d t -> (n s d) h t")).then_inc(done, 16)

                    def m_rows(g, u, reg):
                        sp.wait_ge(m_chain, M_STEPS * (g + 1))
                        sp.dma_start(m_scr[reg].rearrange("n p c -> (n p) c"), mT[:]).then_inc(m_stored, 16)
                        sp.wait_ge(m_stored, 16 * (g + 1))
                        src = m_scr[reg].rearrange("n (b c) (s r) -> b (n s) c r", b=4, s=PARTS)
                        for blk in range(4):
                            dst = Qa[M_ROW:M_ROW + PARTS, u, :, :].rearrange(
                                "s h (i b r) -> s b (h i) r", b=4, r=32)[:, blk]
                            sp.dma_start(dst, src[blk]).then_inc(mrow_loaded[u], 16)

                    sp.wait_ge(pads_made, 5)
                    load_parts(Qx[:, 0], Kx[:, 0], bass.ds(0, 1), xop_loaded[0])
                    load_parts(Qx[:, 1], Kx[:, 1], bass.ds(1, 1), xop_loaded[1])
                    load_parts(Qa[:, 0], Ka[:, 0], bass.ds(0, 1), sop_loaded[0])
                    m_rows(0, 0, bass.ds(0, 1))

                    def store_o(n, half):
                        sp.wait_ge(o_read, 2 * n + half + 1 + ONE)
                        sp.dma_start(o_scr[bass.ds(n, 1), :, CHUNK * half:CHUNK * (half + 1)].rearrange(
                            "n p t -> (n p) t"), Os[:, half, :]).then_inc(o_stored[half], 16)

                    def group(n, u, last):
                        if last < 1:
                            sp.wait_ge(mx_read, CPG * (n + 1))
                            load_parts(Qx[:, u], Kx[:, u], bass.ds(n + 2, 1), xop_loaded[u])
                        if last < 2:
                            sp.wait_ge(s_ready, SPG * n + ONE)
                            load_parts(Qa[:, 1 - u], Ka[:, 1 - u], bass.ds(n + 1, 1), sop_loaded[1 - u])
                        store_o(n, 0)
                        if last < 2:
                            m_rows(n + 1, 1 - u, bass.ds(n + 1, 1))
                        store_o(n, 1)

                    with sp.Fori(0, GROUPS // 2 - 1) as i:
                        for u in range(2):
                            group(2 * i + u, u, 0)
                    group(GROUPS - 2, 0, 1)
                    group(GROUPS - 1, 1, 2)
                    for half in range(2):
                        sp.wait_ge(o_stored[half], 16 * GROUPS + ONE)

                @block.gpsimd
                def _(pool):
                    pool.memset(Qx[:], 0.0).then_inc(pads_made, 1)
                    pool.memset(Kx[:], 0.0).then_inc(pads_made, 1)
                    pool.memset(Qa[:], 0.0).then_inc(pads_made, 1)
                    pool.memset(Ka[:], 1.0).then_inc(pads_made, 1)
                    pool.memset(tri[:], 0.0).then_inc(consts_made, 1)
                    pool.wait_ge(consts_made, 5)
                    pool.affine_select(out=tri[:, CHUNK - P:CHUNK], in_=tri[:, CHUNK - P:CHUNK], compare_op=ALU.is_ge,
                                       fill=-BIG, base=0, pattern=[[-1, P]], channel_multiplier=1).then_inc(pads_made, 1)

                    def group(n):
                        for r, k in enumerate(DIAG_UNITS):
                            step = UNITS[k][1][1][3]
                            for hh in range(GH):
                                wait_alone(pool, exp_done, SPG * n + GH * k + hh + 1 + FREE, pads_made)
                                diag = probs[:, k % 2, hh, 0:2 * step].rearrange("p (a c) -> p a c", a=2)[:, :, 0:P]
                                pool.affine_select(out=diag, in_=diag, compare_op=ALU.is_ge, fill=0.0, base=0,
                                                   pattern=[[0, 2], [1, P]], channel_multiplier=-1).then_inc(masked, 1)

                    with pool.Fori(0, GROUPS) as n:
                        group(n)

                @block.scalar
                def _(act):
                    act.sem_inc(exp_done, FREE)

                    def evacuate(n, half):
                        act.wait_ge(pv_done, NU * n + (2 if half == 0 else NU) + 1 + ONE)
                        act.wait_ge(o_stored[half], 16 * n + ONE)
                        act.activation(Os[:, half, :], ps[:, O_BANK, :], ACT.Copy).then_inc(o_read, 1)

                    def group(n):
                        for k, (half, tiles, width) in enumerate(UNITS):
                            act.wait_ge(pv_done, NU * n + k + ONE)
                            for hh in range(GH):
                                e = GH * k + hh
                                act.wait_ge(s_ready, SPG * n + e + 1 + ONE)
                                bank = S_BANK + 2 * (e % 2)
                                act.activation(probs[:, k % 2, hh, 0:width],
                                               ps[:, bank:bank + 2, :].rearrange("p a c -> p (a c)")[:, 0:width],
                                               ACT.Exp, scale=SM_SCALE).then_inc(exp_done, 1)
                                if (k, hh) == (3, 1):
                                    evacuate(n, 0)
                        evacuate(n, 1)

                    with act.Fori(0, GROUPS) as n:
                        group(n)

                @block.tensor
                def _(pe):
                    pe.sem_inc(pv_done, 2)
                    pe.wait_ge(pads_made, 5)

                    def max_chunk(base, f, u, load):
                        i, part, hh, c0, c1 = MAXC[f]
                        if f == 0:
                            pe.wait_ge(xop_loaded[u], load)
                        if not (isinstance(base, int) and base + f < X_SLOTS):
                            pe.wait_ge(mx_read, base + f + 1 - X_SLOTS)
                        pe.matmul(ps[:, X_BANK + f % X_SLOTS, 0:c1 - c0], Qx[:, u, hh, P * i:P * (i + 1)],
                                  Kx[:, u, hh, c0:c1], start=True, stop=True).then_inc(mx_ready, 1)

                    def products(n, u, k):
                        half, tiles, width = UNITS[k]
                        if k == 0:
                            pe.wait_ge(o_read, 2 * n + ONE)
                            pe.wait_ge(v_staged, n + 3)
                        if k == 2:
                            pe.wait_ge(o_read, 2 * n + 1 + ONE)
                        if k in DIAG_UNITS:
                            pe.wait_ge(masked, MPG * n + GH * (DIAG_UNITS.index(k) + 1))
                        else:
                            pe.wait_ge(exp_done, SPG * n + GH * (k + 1) + FREE)
                        for j, q0, w, off in tiles:
                            for hh in range(GH):
                                mm = pe.matmul(ps[32 * hh:32 * hh + VW, O_BANK, q0 - CHUNK * half:q0 - CHUNK * half + w],
                                               Vg[:, u, j, hh, :], probs[:, k % 2, hh, off:off + w],
                                               start=(j == 0), stop=(j == 4 * half + 3), skip_group_check=True)
                        mm.then_inc(pv_done, 1)

                    def scores(n, u, e, load):
                        k, hh = divmod(e, GH)
                        if e == 0:
                            pe.wait_ge(sop_loaded[u], 6 * 16 * load)
                            pe.wait_ge(mrow_loaded[u], 4 * 16 * load)
                        pe.wait_ge(exp_done, SPG * n + e + 1)
                        for j, q0, w, off in UNITS[k][1]:
                            bank = S_BANK + 2 * (e % 2) + off // CHUNK
                            mm = pe.matmul(ps[:, bank, off % CHUNK:off % CHUNK + w], Ka[:, u, hh, P * j:P * (j + 1)],
                                           Qa[:, u, hh, q0:q0 + w], start=True, stop=True)
                        mm.then_inc(s_ready, 1)

                    for f in range(CPG):
                        max_chunk(0, f, 0, 6 * 16)
                    for f in range(AHEAD):
                        max_chunk(CPG, f, 1, 6 * 16)

                    def group(n, u, turn, last):
                        for kind, at in order:
                            if kind == "s":
                                scores(n, u, at, turn + 1)
                                if at % GH == GH - 1 and at >= GH:
                                    products(n, u, at // GH - 1)
                            elif at + AHEAD < CPG and last < 2:
                                max_chunk(CPG * (n + 1), at + AHEAD, 1 - u, 0)
                            elif at + AHEAD >= CPG and last < 1:
                                max_chunk(CPG * (n + 2), at + AHEAD - CPG, u, 6 * 16 * (turn + 2))
                        products(n, u, NU - 1)

                    with pe.Fori(0, GROUPS // 2 - 1) as i:
                        for u in range(2):
                            group(2 * i + u, u, i, 0)
                    group(GROUPS - 2, 0, GROUPS // 2 - 1, 1)
                    group(GROUPS - 1, 1, GROUPS // 2 - 1, 2)

                @block.vector
                def _(dve):
                    dve.memset(ps[:, O_BANK, :], 0.0).then_inc(v_staged, 1)
                    dve.memset(mx[:], -BIG).then_inc(v_staged, 1)
                    dve.tensor_copy(Vg[:, 0, :, :, :], vaug[:, 0, :, :, :]).then_inc(v_staged, 1)
                    dve.wait_ge(v_staged, 3)
                    dve.wait_ge(pads_made, 5)

                    def max_chunk(base, f):
                        i, part, hh, c0, c1 = MAXC[f]
                        w = c1 - c0
                        src = ps[:, X_BANK + f % X_SLOTS, 0:w]
                        if c1 == P * (i + 1):
                            wait_alone(dve, mx_ready, base + f + 1, pads_made)
                        else:
                            dve.wait_ge(mx_ready, base + f + 1)
                        if c1 == P * (i + 1):
                            dve.tensor_tensor_reduce(out=junk[:, f % 4, 0:w], in0=src, in1=tri[:, CHUNK - w:CHUNK], scale=1.0,
                                                     scalar=-BIG, op0=ALU.add, op1=ALU.max,
                                                     accum_out=mx[:, hh, i, 1:2]).then_inc(mx_read, 1)
                        else:
                            dve.tensor_reduce(mx[:, hh, i, 0:1], src, AX.X, ALU.max).then_inc(mx_read, 1)

                    def split_max(g):
                        c = M_STEPS * g
                        dve.wait_ge(mx_read, CPG * (g + 1))
                        dve.tensor_tensor(mm_[:].rearrange("p (h i) -> p h i", h=GH), mx[:, :, :, 0], mx[:, :, :, 1],
                                          ALU.max).then_inc(m_chain, 1)
                        dve.wait_ge(m_chain, c + 1)
                        dve.tensor_scalar(msp[:, 0:32], mm_[:], -1.0, None, ALU.mult).then_inc(m_chain, 1)
                        dve.wait_ge(m_chain, c + 2)
                        dve.scalar_tensor_tensor(out=mr[:], in0=mm_[:], scalar=-1.0, in1=msp[:, 0:32], op0=ALU.mult,
                                                 op1=ALU.subtract).then_inc(m_chain, 1)
                        dve.wait_ge(m_chain, c + 3)
                        dve.tensor_copy(msp[:, 32:64], mr[:]).then_inc(m_chain, 1)
                        dve.wait_ge(m_chain, c + 4)
                        dve.tensor_tensor(msp[:, 64:96], mr[:], msp[:, 32:64], ALU.subtract).then_inc(m_chain, 1)
                        dve.wait_ge(m_chain, c + 5)
                        dve.wait_ge(m_stored, 16 * g)
                        dve.transpose(mT[:], msp[:]).then_inc(m_chain, 1)

                    for f in range(CPG):
                        max_chunk(0, f)
                    split_max(0)
                    for f in range(AHEAD):
                        max_chunk(CPG, f)

                    def group(n, u, last):
                        for f in range(CPG):
                            if f == 12 and last < 2:
                                dve.wait_ge(pv_done, NU * n + 1 + ONE)
                                dve.tensor_copy(Vg[:, 1 - u, :, :, :], vaug[:, bass.ds(n + 1, 1), :, :, :].rearrange(
                                    "p n j h d -> p (n j) h d")).then_inc(v_staged, 1)
                            if f + AHEAD < CPG and last < 2:
                                max_chunk(CPG * (n + 1), f + AHEAD)
                            elif f + AHEAD >= CPG and last < 1:
                                max_chunk(CPG * (n + 2), f + AHEAD - CPG)
                            if f + AHEAD == CPG - 1 and last < 2:
                                split_max(n + 1)

                    with dve.Fori(0, GROUPS // 2 - 1) as i:
                        for u in range(2):
                            group(2 * i + u, u, 0)
                    group(GROUPS - 2, 0, 1)
                    group(GROUPS - 1, 1, 2)

        with ExitStack() as phase:
            def sa(name, shape, dt=F32):
                return phase.enter_context(nc.sbuf_tensor(name, shape, dt))

            ot = sa("ot", [P, HG, CHUNK])
            xc = sa("xc", [P, TPC, D])
            xb = sa("xb", [P, TPC, D])
            rden = sa("rden", [P, 2, HEADS])
            attn = sa("attn", [P, 2, D])
            attnT = sa("attnT", [P, 2, P])
            z = sa("z", [P, TPC, D])
            stats = sa("stats", [P, TPC, 6])
            mv = sa("mv", [P, TPC, 2])
            veps = sa("veps", [P, TPC])
            rstd = sa("rstd", [P, TPC])
            x1 = sa("x1", [P, TPC, D])
            x1b = sa("x1b", [P, TPC, D])
            x1T = sa("x1T", [P, CHUNK])
            gate = sa("gate", [P, FC, CHUNK])
            upv = sa("upv", [P, FC, CHUNK])
            h = sa("h", [P, FC, CHUNK])
            sG = sa("sG", [P, FC, CHUNK])
            sim = sa("sim", [P, 2, 2 * RH * NK])
            V = sa("V", [P, 2, 2 * RH, KPH])
            ixu = sa("ixu", [P, 2, RH, KPH], U32)
            ixf = sa("ixf", [P, 2, RH * KPH])
            ymark = sa("ymark", [P, 2, RH, NK])
            cand = sa("cand", [P, 2, RH, KPH, KPH])
            cmark = sa("cmark", [P, 2, RH, KPH, KPH])
            T = sa("T", [P, 2, RH, KPH])
            EX, EY, EC = 0, RH * XIN, RH * XIN + RH * NK
            shift = sa("shift", [P, 2, EC + RH * NK])
            edge_ab = sa("edge_ab", [P, RH, KPH, KPH])
            edge_a = sa("edge_a", [P, RH * KPH])
            edge_ax = sa("edge_ax", [P, RH * KPH, XIN])
            edge_x = sa("edge_x", [P, 2, RH, XIN])
            picked = sa("picked", [P, RH * KPH, KPH])
            sum_a = sa("sum_a", [P, RH, KPH])
            den = sa("den", [P, RH])
            rz = sa("rz", [P, RH])
            far = sa("far", [P, RH, KPH])
            rest = sa("rest", [P, 2, RH])
            exn = sa("exn", [P, 2, RH, XIN])
            eym = sa("eym", [P, 2, RH, NK])
            A = sa("A", [P, 2, RH, XIN, NK])
            E = sa("E", [P, 2, RH, XIN, NK])
            Wt = sa("Wt", [P, 2, FC, P])
            z2 = sa("z2", [P, TPC, D])
            fin = sa("fin", [P, TPC, D])

            ATTN, ATTNT, Y, X1T, RING, SIM, AT, OUT = 0, (1, 2), (3, 4), 6, (3, 4), (5, 0), 6, (7, 2)
            ROUTE = [("r1", 0), ("r1", 1), ("r2", 0), ("r1", 2), ("r2", 1), ("dense", 0), ("r1", 3), ("wt", 0),
                     ("r2", 2), ("dense", 1), ("r2", 3), ("wt", 1), ("dense", 2), ("z2", 0), ("wt", 2), ("z2", 1),
                     ("dense", 3), ("z2", 2), ("wt", 3), ("z2", 3)]

            with nc.Block() as block:
                @block.sync
                def _(sp):
                    with sp.Fori(0, BATCH) as b:
                        for u in range(2):
                            c = 2 * b + u
                            sp.wait_ge(oT_ready, TPC * c + ONE)
                            sp.dma_start(ot[:], o_scr[bass.ds(b * HG, HG), :, CHUNK * u:CHUNK * (u + 1)].rearrange(
                                "g p t -> p g t")).then_inc(ot_loaded, 16)
                            sp.wait_ge(xb_ready, c + ONE)
                            sp.dma_start(xc[:], x_chunks[bass.ds(c, 1)].rearrange(
                                "c p t d -> (c p) t d")).then_inc(xc_loaded, 16)

                @block.gpsimd
                def _(pool):
                    def route_shift(c, t):
                        m, s = TPC * c + t, t % 2
                        pool.wait_ge(cand_ready, m + 1)
                        pool.tensor_tensor(shift[:, s, EX:EY].rearrange("p (h x) -> p h x", h=RH),
                                           sim[:, s, 0:RH * NK].rearrange("p (h x) -> p h x", h=RH)[:, :, 0:XIN],
                                           V[:, s, 0:RH, 0:1].broadcast_to([P, RH, XIN]), ALU.subtract)
                        pool.tensor_tensor(shift[:, s, EY:EC].rearrange("p (h y) -> p h y", h=RH),
                                           sim[:, s, RH * NK:].rearrange("p (h y) -> p h y", h=RH),
                                           V[:, s, RH:2 * RH, 0:1].broadcast_to([P, RH, NK]), ALU.subtract)
                        pool.tensor_tensor(shift[:, s, EC:].rearrange("p (h y) -> p h y", h=RH),
                                           cand[:, s].rearrange("p h a b -> p h (a b)"),
                                           T[:, s, :, 0:1].broadcast_to([P, RH, NK]), ALU.subtract).then_inc(shifted, 1)

                    def spread(c, t):
                        m, s = TPC * c + t, t % 2
                        pool.wait_ge(edge_ready, m + 1)
                        if t >= 2:
                            pool.wait_ge(AT_ready, m - 1)
                        pool.tensor_tensor(A[:, s], sim[:, s, RH * NK:].rearrange("p (h o y) -> p h o y", h=RH, o=1)
                                           .broadcast_to([P, RH, XIN, NK]),
                                           edge_x[:, s].unsqueeze(3).broadcast_to([P, RH, XIN, NK]), ALU.subtract)
                        pool.tensor_tensor(E[:, s], eym[:, s].unsqueeze(2).broadcast_to([P, RH, XIN, NK]),
                                           exn[:, s].unsqueeze(3).broadcast_to([P, RH, XIN, NK]),
                                           ALU.mult).then_inc(de_ready, 1)

                    with pool.Fori(0, CHUNKS) as c:
                        pool.wait_ge(xc_loaded, 16 * c + 16)
                        pool.wait_ge(z_done, TPC * c + ONE)
                        pool.tensor_tensor(xb[:], xc[:], bo_row[:].unsqueeze(1).broadcast_to([P, TPC, D]),
                                           ALU.add).then_inc(xb_ready, 1)
                        pool.wait_ge(var_ready, c + 1)
                        pool.tensor_tensor(rstd[:], veps[:], mhalf[:], ALU.pow).then_inc(rstd_ready, 1)
                        pool.wait_ge(x1_ready, c + 1)
                        pool.tensor_tensor(x1b[:], x1[:], bd_row[:].unsqueeze(1).broadcast_to([P, TPC, D]),
                                           ALU.add).then_inc(x1b_ready, 1)
                        route_shift(c, 0)
                        route_shift(c, 1)
                        for f in range(FC):
                            pool.wait_ge(ffn_read, 3 * FC * c + 2 * f + 2 + FREE)
                            pool.wait_ge(out_ready, TPC * c + ONE)
                            pool.tensor_tensor(h[:, f, :], gate[:, f, :], upv[:, f, :], ALU.mult).then_inc(h_ready, 1)
                        spread(c, 0)
                        route_shift(c, 2)
                        spread(c, 1)
                        route_shift(c, 3)
                        spread(c, 2)
                        spread(c, 3)
                        pool.wait_ge(var2_ready, c + 1)
                        pool.tensor_tensor(rstd[:], veps[:], mhalf[:], ALU.pow).then_inc(rstd2_ready, 1)

                @block.scalar
                def _(act):
                    act.sem_inc(ffn_read, FREE)

                    def copy_sim(c, t):
                        act.wait_ge(sim_ready, TPC * c + t + 1)
                        if t >= 2:
                            act.wait_ge(de_ready, TPC * c + t - 1)
                        act.activation(sim[:, t % 2, :], ps[:, SIM[t % 2], :], ACT.Copy).then_inc(sim_copied, 1)

                    def exps(c, t):
                        act.wait_ge(shifted, TPC * c + t + 1)
                        act.activation(shift[:, t % 2, :], shift[:, t % 2, :], ACT.Exp).then_inc(exps_ready, 1)

                    with act.Fori(0, CHUNKS) as c:
                        for t in range(TPC):
                            act.wait_ge(attnT_ready, TPC * c + t + 1)
                            act.activation(attnT[:, t % 2, :], ps[:, ATTNT[t % 2], 0:P],
                                           ACT.Copy).then_inc(attnT_copied, 1)
                        act.wait_ge(x1T_ready, c + 1)
                        act.activation(x1T[:], ps[:, X1T, :], ACT.Copy).then_inc(x1T_copied, 1)
                        copy_sim(c, 0)
                        copy_sim(c, 1)
                        for k in range(3 * FC):
                            act.wait_ge(ffn_ready, 3 * FC * c + k + 1)
                            src = ps[:, RING[k % 2], :]
                            if k < 2 * FC:
                                f = k // 2
                                act.wait_ge(h_ready, FC * c + ONE)
                                act.activation((gate if k % 2 == 0 else upv)[:, f, :], src,
                                               ACT.Silu if k % 2 == 0 else ACT.Identity,
                                               bias=bgu[:, k % 2, f:f + 1]).then_inc(ffn_read, 1)
                            else:
                                act.wait_ge(Wt_ready, TPC * c + ONE)
                                act.activation(sG[:, k - 2 * FC, :], src, ACT.Silu).then_inc(ffn_read, 1)
                        exps(c, 0)
                        exps(c, 1)
                        copy_sim(c, 2)
                        exps(c, 2)
                        copy_sim(c, 3)
                        exps(c, 3)
                        act.wait_ge(fin_ready, c + 1)
                        act.dma_start(out_chunks[bass.ds(c, 1)].rearrange("c p t d -> (c p) t d"),
                                      fin[:]).then_inc(out_stored, 16)
                    act.wait_ge(out_stored, 16 * CHUNKS + ONE)

                @block.tensor
                def _(pe):
                    def sims(c, t):
                        if t == 1:
                            pe.wait_ge(attn_ready, TPC * c + TPC + ONE)
                        if t >= 2:
                            pe.wait_ge(sim_copied, TPC * c + t - 1 + ONE)
                        pe.matmul(ps[:, SIM[t % 2], :], x1T[:, P * t:P * (t + 1)],
                                  Wsim[:].rearrange("p a b -> p (a b)"), start=True, stop=True).then_inc(sim_ready, 1)

                    def combine(c, t):
                        m, s = TPC * c + t, t % 2
                        pe.wait_ge(A_ready, m + 1)
                        pe.wait_ge(Wt_ready, m + ONE)
                        Af = A[:, s].rearrange("p h x y -> p h (x y)")
                        for e in range(FC):
                            for hd in range(RH):
                                mm = pe.matmul(ps[:, AT, P * e:P * (e + 1)], Af[:, hd, P * e:P * (e + 1)], ident[:],
                                               start=(hd == 0), stop=(hd == RH - 1))
                        mm.then_inc(AT_ready, 1)

                    def output(c, t):
                        m, s = TPC * c + t, t % 2
                        dst = ps[:, OUT[t % 2], 0:P]
                        pe.wait_ge(h_ready, FC * c + FC + ONE)
                        if t >= 2:
                            pe.wait_ge(z2_done, m - 1)
                        for f in range(FC):
                            pe.matmul(dst, h[:, f, P * t:P * (t + 1)], Wd_sb[:, f, :], start=(f == 0), stop=False)
                        pe.wait_ge(Wt_ready, m + 1 + ONE)
                        for e in range(FC):
                            mm = pe.matmul(dst, Wt[:, s, e, :], up_sb[:, e, :], start=False, stop=(e == FC - 1))
                        mm.then_inc(out_ready, 1)

                    with pe.Fori(0, CHUNKS) as c:
                        pe.wait_ge(ot_loaded, 16 * c + 16)
                        pe.wait_ge(sim_copied, TPC * c + ONE)
                        for step in range(TPC + 2):
                            if step < TPC:
                                pe.wait_ge(attn_ready, TPC * c + step + ONE)
                                for g in range(HG):
                                    mm = pe.transpose(ps[:, ATTN, P * g:P * (g + 1)], ot[:, g, P * step:P * (step + 1)], ident[:])
                                mm.then_inc(oT_ready, 1)
                            t = step - 1
                            if 0 <= t < TPC:
                                pe.wait_ge(attn_ready, TPC * c + t + 1 + ONE)
                                pe.transpose(ps[:, ATTNT[t % 2], 0:P], attn[:, t % 2, :],
                                             ident[:]).then_inc(attnT_ready, 1)
                            t = step - 2
                            if 0 <= t < TPC:
                                pe.wait_ge(attnT_copied, TPC * c + t + 1)
                                if t >= 2:
                                    pe.wait_ge(z_done, TPC * c + t - 1 + ONE)
                                pe.matmul(ps[:, Y[t % 2], 0:P], attnT[:, t % 2, :], WoT[:],
                                          start=True, stop=True).then_inc(y_ready, 1)
                        pe.wait_ge(x1_ready, c + 1)
                        for t in range(TPC):
                            mm = pe.transpose(ps[:, X1T, P * t:P * (t + 1)], x1[:, t, :], ident[:])
                        mm.then_inc(x1T_ready, 1)
                        pe.wait_ge(x1T_copied, c + 1)
                        sims(c, 0)
                        sims(c, 1)
                        for k in range(3 * FC):
                            pe.wait_ge(ffn_read, 3 * FC * c + k + 1)
                            if k < 2 * FC:
                                w = (Wg_sb if k % 2 == 0 else Wu_sb)[:, P * (k // 2):P * (k // 2 + 1)]
                            else:
                                w = downT[:, P * (k - 2 * FC):P * (k - 2 * FC + 1)]
                            pe.matmul(ps[:, RING[k % 2], :], w, x1T[:], start=True, stop=True).then_inc(ffn_ready, 1)
                        sims(c, 2)
                        sims(c, 3)
                        for t in range(TPC):
                            combine(c, t)
                            output(c, t)

                @block.vector
                def _(dve):
                    steps = [0]

                    def link(ins, c, alone=False):
                        steps[0] += 1
                        ins.then_inc(c_chain, 1)
                        if alone:
                            wait_alone(dve, c_chain, LINKS * c + steps[0], consts_made)
                        else:
                            dve.wait_ge(c_chain, LINKS * c + steps[0])

                    def r1(c, t):
                        m, s = TPC * c + t, t % 2
                        wait_alone(dve, sim_copied, m + 1 + ONE, consts_made)
                        for g in range(2 * RH):
                            last = dve.max(V[:, s, g, :], sim[:, s, NK * g:NK * (g + 1)])
                        link(last, c, alone=True)
                        for hd in range(RH):
                            dve.max_index(ixu[:, s, hd, :], V[:, s, hd, :], sim[:, s, NK * hd:NK * (hd + 1)])
                        for hd in range(RH):
                            dve.match_replace(ymark[:, s, hd, :], V[:, s, RH + hd, :],
                                              sim[:, s, NK * (RH + hd):NK * (RH + hd + 1)], BIG)
                        link(dve.tensor_tensor(cand[:, s], V[:, s, 0:RH, :].unsqueeze(3).broadcast_to([P, RH, KPH, KPH]),
                                               V[:, s, RH:2 * RH, :].unsqueeze(2).broadcast_to([P, RH, KPH, KPH]),
                                               ALU.add), c, alone=True)
                        for hd in range(RH):
                            last = dve.max(T[:, s, hd, :], cand[:, s, hd].rearrange("p a b -> p (a b)"))
                        last.then_inc(cand_ready, 1)
                        wait_alone(dve, cand_ready, m + 1, consts_made)
                        for hd in range(RH):
                            dve.match_replace(cmark[:, s, hd].rearrange("p a b -> p (a b)"), T[:, s, hd, :],
                                              cand[:, s, hd].rearrange("p a b -> p (a b)"), BIG)
                        link(dve.tensor_copy(ixf[:, s, :], ixu[:, s].rearrange("p h a -> p (h a)")), c, alone=True)

                    def r2(c, t):
                        m, s = TPC * c + t, t % 2
                        link(dve.tensor_scalar(edge_ab[:], cmark[:, s], MARKED, FAR, ALU.is_lt, ALU.mult), c)
                        link(dve.tensor_tensor(edge_ab[:], edge_ab[:],
                                               V[:, s, RH:2 * RH, :].unsqueeze(2).broadcast_to([P, RH, KPH, KPH]),
                                               ALU.add), c)
                        dve.tensor_reduce(edge_a[:], edge_ab[:].rearrange("p h a b -> p (h a) b"), AX.X, ALU.min)
                        link(dve.tensor_tensor(edge_ax[:], ixf[:, s, :].unsqueeze(2).broadcast_to([P, RH * KPH, XIN]),
                                               iota8[:].unsqueeze(1).broadcast_to([P, RH * KPH, XIN]),
                                               ALU.not_equal), c)
                        link(dve.scalar_tensor_tensor(out=edge_ax[:], in0=edge_ax[:], scalar=FAR,
                                                      in1=edge_a[:].unsqueeze(2).broadcast_to([P, RH * KPH, XIN]),
                                                      op0=ALU.mult, op1=ALU.add), c)
                        dve.tensor_reduce(edge_x[:, s], edge_ax[:].rearrange("p (h a) x -> p h x a", h=RH), AX.X, ALU.min)
                        dve.wait_ge(exps_ready, m + 1)
                        link(dve.scalar_tensor_tensor(out=picked[:], in0=cmark[:, s].rearrange("p h a b -> p (h a) b"),
                                                      scalar=MARKED,
                                                      in1=shift[:, s, EC:].rearrange("p (a b) -> p a b", b=KPH),
                                                      op0=ALU.is_ge, op1=ALU.mult), c)
                        dve.scalar_tensor_tensor(out=eym[:, s].rearrange("p h y -> p (h y)"),
                                                 in0=ymark[:, s].rearrange("p h y -> p (h y)"), scalar=MARKED,
                                                 in1=shift[:, s, EY:EC], op0=ALU.is_ge, op1=ALU.mult)
                        link(dve.tensor_reduce(sum_a[:].rearrange("p h a -> p (h a)"), picked[:], AX.X, ALU.add), c)
                        dve.tensor_reduce(den[:], sum_a[:], AX.X, ALU.add)
                        link(dve.scalar_tensor_tensor(out=far[:].rearrange("p h a -> p (h a)"), in0=ixf[:, s, :],
                                                      scalar=float(XIN), in1=sum_a[:].rearrange("p h a -> p (h a)"),
                                                      op0=ALU.is_ge, op1=ALU.mult), c)
                        dve.tensor_reduce(rest[:, s, :], far[:], AX.X, ALU.add)
                        link(dve.reciprocal(rz[:], den[:]), c)
                        dve.tensor_tensor(rest[:, s, :], rest[:, s, :], rz[:], ALU.mult)
                        dve.tensor_tensor(exn[:, s], shift[:, s, EX:EY].rearrange("p (h x) -> p h x", h=RH),
                                          rz[:].unsqueeze(2).broadcast_to([P, RH, XIN]), ALU.mult).then_inc(edge_ready, 1)

                    def dense(c, t):
                        m, s = TPC * c + t, t % 2
                        dve.wait_ge(de_ready, m + 1)
                        flat = A[:, s].rearrange("p h x y -> p (h x y)")
                        link(dve.scalar_tensor_tensor(out=flat, in0=flat, scalar=0.0,
                                                      in1=E[:, s].rearrange("p h x y -> p (h x y)"),
                                                      op0=ALU.is_ge, op1=ALU.mult), c)
                        end = A[:, s, :, XIN - 1, NK - 1]
                        dve.tensor_tensor(end, end, rest[:, s, :], ALU.add).then_inc(A_ready, 1)

                    def wt(c, t):
                        m, s = TPC * c + t, t % 2
                        dve.wait_ge(AT_ready, m + 1)
                        if t == 0:
                            dve.wait_ge(ffn_read, 3 * FC * (c + 1) + FREE)
                        if t >= 2:
                            dve.wait_ge(out_ready, m - 1 + ONE)
                        dve.tensor_tensor(Wt[:, s], ps[:, AT, :].rearrange("p (e t) -> p e t", e=FC),
                                          sG[:, :, P * t:P * (t + 1)], ALU.mult).then_inc(Wt_ready, 1)

                    def moments(c, src, t):
                        link(dve.bn_stats(stats[:, t, :], src[:, t, :]), c, alone=True)
                        dve.bn_aggr(mv[:, t, :], stats[:, t, :]).then_inc(mv_done, 1)

                    def zed2(c, t):
                        m = TPC * c + t
                        dve.wait_ge(out_ready, m + 1 + ONE)
                        dve.wait_ge(x1b_ready, c + 1)
                        dve.tensor_tensor(z2[:, t, :], ps[:, OUT[t % 2], 0:P], x1b[:, t, :],
                                          ALU.add).then_inc(z2_done, 1)
                        dve.wait_ge(z2_done, m + 1)
                        moments(c, z2, t)

                    with dve.Fori(0, CHUNKS) as c:
                        for step in range(TPC + 2):
                            if step < TPC:
                                s = step % 2
                                dve.wait_ge(oT_ready, TPC * c + step + 1 + ONE)
                                src = ps[:, ATTN, :].rearrange("p (h r) -> p h r", r=32)
                                link(dve.reciprocal(rden[:, s, :], src[:, :, DH]), c)
                                dve.tensor_tensor(attn[:, s, :].rearrange("p (h d) -> p h d", d=DH), src[:, :, 0:DH],
                                                  rden[:, s, :].unsqueeze(2).broadcast_to([P, HEADS, DH]),
                                                  ALU.mult).then_inc(attn_ready, 1)
                            t = step - 2
                            if 0 <= t < TPC:
                                dve.wait_ge(y_ready, TPC * c + t + 1)
                                dve.wait_ge(xb_ready, c + 1 + ONE)
                                dve.tensor_tensor(z[:, t, :], ps[:, Y[t % 2], 0:P],
                                                  xb[:, t, :], ALU.add).then_inc(z_done, 1)
                                dve.wait_ge(z_done, TPC * c + t + 1 + ONE)
                                moments(c, z, t)
                        dve.wait_ge(mv_done, 2 * TPC * c + TPC)
                        dve.tensor_scalar(veps[:], mv[:, :, 1], EPS, None, ALU.add).then_inc(var_ready, 1)
                        dve.wait_ge(rstd_ready, c + 1)
                        for t in range(TPC):
                            last = dve.tensor_scalar(x1[:, t, :], z[:, t, :], mv[:, t, 0:1], rstd[:, t:t + 1],
                                                     ALU.subtract, ALU.mult)
                        last.then_inc(x1_ready, 1)
                        for kind, t in ROUTE:
                            {"r1": r1, "r2": r2, "dense": dense, "wt": wt, "z2": zed2}[kind](c, t)
                        dve.wait_ge(mv_done, 2 * TPC * (c + 1))
                        dve.tensor_scalar(veps[:], mv[:, :, 1], EPS, None, ALU.add).then_inc(var2_ready, 1)
                        dve.wait_ge(rstd2_ready, c + 1)
                        dve.wait_ge(out_stored, 16 * c + ONE)
                        for t in range(TPC):
                            last = dve.tensor_scalar(fin[:, t, :], z2[:, t, :], mv[:, t, 0:1], rstd[:, t:t + 1],
                                                     ALU.subtract, ALU.mult)
                        last.then_inc(fin_ready, 1)
                    assert steps[0] == LINKS, steps[0]


_INS = ["L0_attn_x", "L0_attn_W_qkv", "L0_attn_b_qkv", "L0_attn_W_o", "L0_attn_b_o", "L0_ffn_Wg", "L0_ffn_bg",
        "L0_ffn_Wu", "L0_ffn_bu", "L0_ffn_Wd", "L0_ffn_bd", "L0_ffn_Wq", "L0_ffn_keys", "L0_ffn_down_embed",
        "L0_ffn_up_embed"]
_OUTS = [((4, 1024, 128), "float32")]


def kernel(**inputs):
    import numpy as _np
    import concourse.bacc as _bacc
    from concourse import mybir as _mybir
    from concourse.bass_utils import run_bass_kernel_spmd as _run

    nc = _bacc.Bacc("TRN2", target_bir_lowering=False, num_devices=1)
    arrays, args = {}, []
    for name in _INS:
        a = _np.ascontiguousarray(inputs[name])
        arrays[f"in_{name}_dram"] = a
        args.append(nc.dram_tensor(f"in_{name}_dram", a.shape, _mybir.dt.from_np(a.dtype), kind="ExternalInput").ap())
    for i, (shape, dtype) in enumerate(_OUTS):
        dt = _mybir.dt.from_np(_np.dtype(dtype))
        args.append(nc.dram_tensor(f"out_{i}_dram", shape, dt, kind="ExternalOutput").ap())
    build(nc, *args)
    r = _run(nc, [arrays], core_ids=[0])
    got = tuple(r.results[0][f"out_{i}_dram"] for i in range(len(_OUTS)))
    return got[0]
```

```python
from contextlib import ExitStack

import concourse.bass as bass
from concourse import mybir

F32 = mybir.dt.float32
BF16 = mybir.dt.bfloat16
U32 = mybir.dt.uint32
ALU = mybir.AluOpType
ACT = mybir.ActivationFunctionType
AX = mybir.AxisListType

P = 128
BATCH, SEQ, D = 4, 1024, 128
HEADS, DH = 16, 8
TOKENS = BATCH * SEQ
TILES = TOKENS // P
CHUNK = 512
CHUNKS = TOKENS // CHUNK
TPC = CHUNK // P
HG = 4
GH = HEADS // HG
GROUPS = BATCH * HG
PARTS = 3
SPLIT_ROWS = PARTS * PARTS * DH
M_ROW = SPLIT_ROWS
VW = DH + 1
F = 512
FC = F // P
NEXP = 512
NK = 64
RH = 4
KPH = 8
XIN = NEXP // NK
EPS = 1e-5
SM_SCALE = float(DH) ** -0.5
BIG = 3.0e38
MARKED = 2.9e38
FAR = 1.0e38

UNITS = []
for _half, _tiles in ((0, (0, 1)), (0, (2, 3)), (1, (0, 1)), (1, (2, 3)), (1, (4, 5)), (1, (6, 7))):
    _at, _off = [], 0
    for _j in _tiles:
        _q0 = max(P * _j, CHUNK * _half)
        _w = CHUNK * (_half + 1) - _q0
        _at.append((_j, _q0, _w, _off))
        _off += _w
    UNITS.append((_half, _at, _off))
NU = len(UNITS)
DIAG_UNITS = [k for k, (h, at, w) in enumerate(UNITS) if at[0][0] >= 4 * h]
SPG = NU * GH
MPG = len(DIAG_UNITS) * GH

MAXC = []
for _i in range(SEQ // P - 1, -1, -1):
    _end = P * (_i + 1)
    for _part, (_c0, _c1) in enumerate([(0, CHUNK), (CHUNK, _end)] if _end > CHUNK else [(0, _end)]):
        for _hh in range(GH):
            MAXC.append((_i, _part, _hh, _c0, _c1))
CPG = len(MAXC)
AHEAD = 16
X_SLOTS = 3
FREE = 2
ONE = 1
S_BANK, O_BANK, X_BANK = 0, 4, 5
M_STEPS = 6
LINKS = 52


def wait_alone(eng, signal, value, done):
    if not isinstance(value, int):
        value = eng.to_reg(value)
    eng.wait_ge(done, 1)
    eng.wait_ge(signal, value)


def interleave():
    order, ta, td, e, f = [], 0.0, 0.0, 0, 0
    while e < SPG or f < CPG:
        if f >= CPG or (e < SPG and ta <= td):
            order.append(("s", e))
            ta += UNITS[e // GH][2] * 0.83 + 120
            e += 1
        else:
            order.append(("x", f))
            i, part, hh, c0, c1 = MAXC[(f + AHEAD) % CPG]
            td += (c1 - c0) * 1.04 + 80
            f += 1
    return order


def build(nc, x, W_qkv, b_qkv, W_o, b_o, Wg, bg, Wu, bu, Wd, bd, Wq, keys, down, up, out):
    order = interleave()
    q_scr = nc.dram_tensor("q_scr", [GROUPS, GH, 5, DH, SEQ], BF16).ap()
    k_scr = nc.dram_tensor("k_scr", [GROUPS, GH, PARTS, DH, SEQ], BF16).ap()
    m_scr = nc.dram_tensor("m_scr", [GROUPS, P, PARTS * 32], BF16).ap()
    o_scr = nc.dram_tensor("o_scr", [GROUPS, P, SEQ], F32).ap()

    with ExitStack() as ctx:
        def sb(name, shape, dt=F32):
            return ctx.enter_context(nc.sbuf_tensor(name, shape, dt))

        def sem(name):
            return ctx.enter_context(nc.semaphore(name))

        ps = ctx.enter_context(nc.psum_tensor("ps", [P, 8, 512], F32))

        ident = sb("ident", [P, P])
        WqkvT = sb("WqkvT", [P, 3, P])
        WoT = sb("WoT", [P, P])
        downT = sb("downT", [P, NEXP])
        Wsim = sb("Wsim", [P, 4, P])
        Wg_sb = sb("Wg_sb", [P, F])
        Wu_sb = sb("Wu_sb", [P, F])
        Wd_sb = sb("Wd_sb", [P, FC, D])
        up_sb = sb("up_sb", [P, FC, D])
        bqk = sb("bqk", [P, 2])
        bgu = sb("bgu", [P, 2, FC])
        bv_row = sb("bv_row", [P, D])
        bo_row = sb("bo_row", [P, D])
        bd_row = sb("bd_row", [P, D])
        iota8 = sb("iota8", [P, XIN])
        mhalf = sb("mhalf", [P, TPC])

        x_loaded = [sem(f"x_loaded{u}") for u in range(2)]
        wqkv_loaded = sem("wqkv_loaded")
        prep_loaded = sem("prep_loaded")
        wts_loaded = sem("wts_loaded")
        kbd_zeroed = sem("kbd_zeroed")
        consts_made = sem("consts_made")
        wT_ready = sem("wT_ready")
        wT_read = sem("wT_read")
        xT_ready = sem("xT_ready")
        xT_read = sem("xT_read")
        qk_ready = sem("qk_ready")
        v_ready = sem("v_ready")
        q_read = sem("q_read")
        v_read = sem("v_read")
        r_made = sem("r_made")
        p2_made = sem("p2_made")
        p3_made = sem("p3_made")
        qk_stored = [sem(f"qk_stored{u}") for u in range(2)]
        pads_made = sem("pads_made")
        xop_loaded = [sem(f"xop_loaded{u}") for u in range(2)]
        sop_loaded = [sem(f"sop_loaded{u}") for u in range(2)]
        mrow_loaded = [sem(f"mrow_loaded{u}") for u in range(2)]
        mx_ready = sem("mx_ready")
        mx_read = sem("mx_read")
        m_chain = sem("m_chain")
        m_stored = sem("m_stored")
        v_staged = sem("v_staged")
        s_ready = sem("s_ready")
        exp_done = sem("exp_done")
        masked = sem("masked")
        pv_done = sem("pv_done")
        o_read = sem("o_read")
        o_stored = [sem(f"o_stored{h}") for h in range(2)]
        ot_loaded = sem("ot_loaded")
        oT_ready = sem("oT_ready")
        attn_ready = sem("attn_ready")
        attnT_ready = sem("attnT_ready")
        attnT_copied = sem("attnT_copied")
        y_ready = sem("y_ready")
        xb_ready = sem("xb_ready")
        z_done = sem("z_done")
        var_ready = sem("var_ready")
        rstd_ready = sem("rstd_ready")
        x1_ready = sem("x1_ready")
        x1T_ready = sem("x1T_ready")
        x1T_copied = sem("x1T_copied")
        ffn_ready = sem("ffn_ready")
        ffn_read = sem("ffn_read")
        h_ready = sem("h_ready")
        sim_ready = sem("sim_ready")
        sim_copied = sem("sim_copied")
        route_done = sem("route_done")
        cand_ready = sem("cand_ready")
        shifted = sem("shifted")
        exps_ready = sem("exps_ready")
        edge_ready = sem("edge_ready")
        de_ready = sem("de_ready")
        A_ready = sem("A_ready")
        AT_ready = sem("AT_ready")
        Wt_ready = sem("Wt_ready")
        out_ready = sem("out_ready")
        x1b_ready = sem("x1b_ready")
        z2_done = sem("z2_done")
        var2_ready = sem("var2_ready")
        rstd2_ready = sem("rstd2_ready")
        fin_ready = sem("fin_ready")
        out_stored = sem("out_stored")
        c_chain = sem("c_chain")
        mv_done = sem("mv_done")
        mv2_done = sem("mv2_done")
        xc_loaded = sem("xc_loaded")

        x_chunks = x.rearrange("b (h t p) d -> (b h) p t d", h=SEQ // CHUNK, p=P)
        out_chunks = out.rearrange("b (h t p) d -> (b h) p t d", h=SEQ // CHUNK, p=P)
        vaug = sb("vaug", [P, GROUPS, SEQ // P, GH, VW])

        with ExitStack() as phase:
            def sa(name, shape, dt=F32):
                return phase.enter_context(nc.sbuf_tensor(name, shape, dt))

            wqkv_nat = sa("wqkv_nat", [P, 3, P])
            wo_nat = sa("wo_nat", [P, P])
            down_nat = sa("down_nat", [P, FC, D])
            wq_nat = sa("wq_nat", [P, F])
            kbdT = sa("kbdT", [P, 4, P])
            WqT = sa("WqT", [P, 4, P])
            kbd = sa("kbd", [P, 4, P])
            xin = sa("xin", [P, 2, TPC, D])
            xT = sa("xT", [P, 2, CHUNK])
            qf = sa("qf", [P, 2, 2, CHUNK])
            rf = sa("rf", [P, 2, 2, CHUNK])
            qs = sa("qs", [P, 2, 2, PARTS, CHUNK], BF16)

            with nc.Block() as block:
                @block.sync
                def _(sp):
                    for signal in (*qk_stored, v_ready, p3_made, s_ready, *o_stored, o_read, oT_ready, xb_ready, z_done,
                                   out_ready, h_ready, Wt_ready, sim_copied, attn_ready, out_stored,
                                   z2_done):
                        sp.sem_inc(signal, ONE)
                    sp.dma_start(down_nat[:], down.rearrange("(c p) d -> p c d", p=P)).then_inc(prep_loaded, 16)
                    sp.dma_start(wq_nat[:], Wq).then_inc(prep_loaded, 16)
                    sp.dma_start(wo_nat[:], W_o).then_inc(prep_loaded, 16)
                    sp.wait_ge(kbd_zeroed, 1)
                    for p in range(2):
                        for h in range(RH):
                            hl = h % 2
                            sp.dma_start(kbdT[64 * hl:64 * hl + 64, 2 * p + h // 2, 64 * hl:64 * hl + 64],
                                         keys[h, :, p, :]).then_inc(prep_loaded, 16)
                    sp.dma_start(Wg_sb[:], Wg).then_inc(wts_loaded, 16)
                    sp.dma_start(Wu_sb[:], Wu).then_inc(wts_loaded, 16)
                    sp.dma_start(Wd_sb[:], Wd.rearrange("(c p) d -> p c d", p=P)).then_inc(wts_loaded, 16)
                    sp.dma_start(up_sb[:], up.rearrange("(c p) d -> p c d", p=P)).then_inc(wts_loaded, 16)
                    for i, bias in enumerate((bg, bu)):
                        sp.dma_start(bgu[:, i, :], bias.rearrange("(c p) -> p c", p=P),
                                     allow_slow_non_contiguous=True).then_inc(wts_loaded, 16)
                    sp.dma_start(bo_row[:], b_o.rearrange("(o d) -> o d", o=1).broadcast_to([P, D])).then_inc(wts_loaded, 16)
                    sp.dma_start(bd_row[:], bd.rearrange("(o d) -> o d", o=1).broadcast_to([P, D])).then_inc(wts_loaded, 16)
                    with sp.Fori(0, BATCH) as b:
                        for u in range(2):
                            sp.wait_ge(p3_made, 4 * b + 2 * u + 2 + ONE)
                            for s in range(5):
                                dst = q_scr[bass.ds(b * HG, HG), :, s, :, CHUNK * u:CHUNK * (u + 1)]
                                sp.dma_start(dst.rearrange("n h d t -> (n h) d t"),
                                             qs[:, u, 0, s % PARTS, :]).then_inc(qk_stored[u], 16)
                            for s in range(PARTS):
                                dst = k_scr[bass.ds(b * HG, HG), :, s, :, CHUNK * u:CHUNK * (u + 1)]
                                sp.dma_start(dst.rearrange("n h d t -> (n h) d t"),
                                             qs[:, u, 1, s, :]).then_inc(qk_stored[u], 16)
                    for u in range(2):
                        sp.wait_ge(qk_stored[u], 128 * BATCH + ONE)
                    sp.wait_ge(wts_loaded, 16 * 8)

                @block.gpsimd
                def _(pool):
                    pool.memset(ident[:], 0.0).then_inc(consts_made, 1)
                    pool.wait_ge(consts_made, 1)
                    pool.affine_select(out=ident[:], in_=ident[:], compare_op=ALU.not_equal, fill=1.0, base=0,
                                       pattern=[[1, P]], channel_multiplier=-1).then_inc(consts_made, 1)
                    pool.memset(kbdT[:], 0.0).then_inc(kbd_zeroed, 1)
                    pool.memset(vaug[:], 1.0).then_inc(consts_made, 1)
                    pool.memset(mhalf[:], -0.5)
                    pool.iota(iota8[:], pattern=[[1, XIN]], base=0, channel_multiplier=0,
                              allow_small_or_imprecise_dtypes=True).then_inc(consts_made, 1)

                    with pool.Fori(0, BATCH) as b:
                        for u in range(2):
                            for w in range(2):
                                pool.wait_ge(p2_made, 4 * b + 2 * u + w + 1)
                                pool.tensor_tensor(qs[:, u, w, 2, :], rf[:, u, w, :], qs[:, u, w, 1, :],
                                                   ALU.subtract).then_inc(p3_made, 1)

                @block.scalar
                def _(act):
                    act.dma_start(wqkv_nat[:], W_qkv.rearrange("(c p) d -> p c d", p=P)).then_inc(wqkv_loaded, 16)
                    bqkv = b_qkv.rearrange("(w p) -> p w", w=3)
                    act.dma_start(bqk[:], bqkv[:, 0:2], allow_slow_non_contiguous=True).then_inc(wqkv_loaded, 16)
                    act.dma_start(bv_row[:], b_qkv.rearrange("(w d) -> w d", w=3)[2:3, :].broadcast_to([P, D])).then_inc(wqkv_loaded, 16)
                    for u in range(2):
                        act.dma_start(xin[:, u, :, :], x_chunks[u]).then_inc(x_loaded[u], 16)
                    for n, (bank, dst) in enumerate(((0, WqkvT[:, :, :]), (1, WoT[:, :]), (2, downT[:, :]),
                                                     (3, WqT[:, :, :]), (4, kbd[:, :, :]), (5, Wsim[:, :, :]))):
                        act.wait_ge(wT_ready, n + 1)
                        src = ps[:, bank, 0:dst.free_size()]
                        if len(dst.shape) == 3:
                            src = src.rearrange("p (a b) -> p a b", b=P)
                        act.activation(dst, src, ACT.Copy).then_inc(wT_read, 1)
                    act.wait_ge(wqkv_loaded, 48)
                    act.sem_inc(q_read, 2 * FREE)

                    def first_parts(b, more):
                        for u in range(2):
                            if more:
                                act.wait_ge(xT_ready, 2 * b + u + 1)
                                act.dma_start(xin[:, u, :, :], x_chunks[bass.ds(2 * b + u + 2, 1)].rearrange(
                                    "c p t d -> (c p) t d")).then_inc(x_loaded[u], 16)
                            act.wait_ge(qk_stored[u], 128 * b + ONE)
                            for w in range(2):
                                act.wait_ge(qk_ready, 4 * b + 2 * u + w + 1)
                                act.activation(qf[:, u, w, :], ps[:, 2 + 2 * w + u, :], ACT.Identity,
                                               bias=bqk[:, w:w + 1])
                                act.activation(qs[:, u, w, 0, :], ps[:, 2 + 2 * w + u, :], ACT.Identity,
                                               bias=bqk[:, w:w + 1]).then_inc(q_read, 1)

                    with act.Fori(0, BATCH - 1) as b:
                        first_parts(b, True)
                    first_parts(BATCH - 1, False)

                @block.tensor
                def _(pe):
                    pe.wait_ge(consts_made, 2)
                    pe.wait_ge(wqkv_loaded, 48)
                    for w in range(3):
                        mm = pe.transpose(ps[:, 0, P * w:P * (w + 1)], wqkv_nat[:, w, :], ident[:])
                    mm.then_inc(wT_ready, 1)
                    pe.wait_ge(prep_loaded, 16 * 11)
                    pe.transpose(ps[:, 1, 0:P], wo_nat[:], ident[:]).then_inc(wT_ready, 1)
                    for bank, blocks in ((2, [down_nat[:, c, :] for c in range(4)]),
                                         (3, [wq_nat[:, P * c:P * (c + 1)] for c in range(4)]),
                                         (4, [kbdT[:, c, :] for c in range(4)])):
                        for c in range(4):
                            mm = pe.transpose(ps[:, bank, P * c:P * (c + 1)], blocks[c], ident[:])
                        mm.then_inc(wT_ready, 1)
                    pe.wait_ge(wT_read, 5)
                    for c in range(4):
                        mm = pe.matmul(ps[:, 5, P * c:P * (c + 1)], WqT[:, c, :], kbd[:, c, :], start=True, stop=True)
                    mm.then_inc(wT_ready, 1)
                    pe.wait_ge(wT_read, 6)
                    with pe.Fori(0, BATCH) as b:
                        for u in range(2):
                            n = 2 * b + u
                            pe.wait_ge(x_loaded[u], 16 * b + 16)
                            pe.wait_ge(xT_read, n + 1)
                            for t in range(TPC):
                                mm = pe.transpose(ps[:, u, P * t:P * (t + 1)], xin[:, u, t, :], ident[:])
                            mm.then_inc(xT_ready, 1)
                            pe.wait_ge(xT_read, n + 1 + FREE)
                            for w in range(2):
                                pe.wait_ge(q_read, 2 * n + w + 1)
                                pe.matmul(ps[:, 2 + 2 * w + u, :], WqkvT[:, w, :], xT[:, u, :],
                                          start=True, stop=True).then_inc(qk_ready, 1)
                            pe.wait_ge(v_read, n + 1)
                            for t in range(TPC):
                                mm = pe.matmul(ps[:, 6 + u, P * t:P * (t + 1)], xT[:, u, P * t:P * (t + 1)],
                                               WqkvT[:, 2, :], start=True, stop=True)
                            mm.then_inc(v_ready, 1)

                @block.vector
                def _(dve):
                    dve.sem_inc(xT_read, FREE)
                    dve.sem_inc(v_read, FREE)
                    dve.wait_ge(consts_made, 3)
                    dve.wait_ge(wqkv_loaded, 48)
                    with dve.Fori(0, BATCH) as b:
                        for u in range(2):
                            n = 2 * b + u
                            dve.wait_ge(xT_ready, n + 1)
                            dve.wait_ge(v_ready, 2 * b + ONE)
                            dve.tensor_copy(xT[:, u, :], ps[:, u, :]).then_inc(xT_read, 1)
                            for w in range(2):
                                dve.wait_ge(q_read, 2 * n + w + 1 + 2 * FREE)
                                dve.wait_ge(p3_made, 4 * b + ONE)
                                dve.tensor_tensor(rf[:, u, w, :], qf[:, u, w, :], qs[:, u, w, 0, :],
                                                  ALU.subtract).then_inc(r_made, 1)
                                dve.wait_ge(r_made, 2 * n + w + 1)
                                dve.tensor_copy(qs[:, u, w, 1, :], rf[:, u, w, :]).then_inc(p2_made, 1)
                            dve.wait_ge(v_ready, n + 1 + ONE)
                            for t in range(TPC):
                                dst = vaug[:, bass.ds(b * HG, HG), TPC * u + t, :, 0:DH]
                                dd = dve.tensor_tensor(dst, ps[:, 6 + u, P * t:P * (t + 1)].rearrange(
                                    "p (g h d) -> p g h d", g=HG, d=DH), bv_row[:].rearrange(
                                    "p (g h d) -> p g h d", g=HG, d=DH), ALU.add)
                            dd.then_inc(v_read, 1)

        with ExitStack() as phase:
            def sa(name, shape, dt=F32):
                return phase.enter_context(nc.sbuf_tensor(name, shape, dt))

            Qx = sa("Qx", [P, 2, GH, SEQ], BF16)
            Kx = sa("Kx", [P, 2, GH, SEQ], BF16)
            Qa = sa("Qa", [P, 2, GH, SEQ], BF16)
            Ka = sa("Ka", [P, 2, GH, SEQ], BF16)
            probs = sa("probs", [P, 2, GH, 2 * CHUNK])
            Vg = sa("Vg", [P, 2, SEQ // P, GH, VW])
            Os = sa("Os", [P, 2, CHUNK])
            tri = sa("tri", [P, CHUNK])
            junk = sa("junk", [P, 4, CHUNK], BF16)
            mx = sa("mx", [P, GH, SEQ // P, 2])
            mm_ = sa("rowmax", [P, 32])
            mr = sa("mr", [P, 32])
            msp = sa("msp", [P, PARTS * 32], BF16)
            mT = sa("mT", [P, PARTS * 32], BF16)

            with nc.Block() as block:
                @block.sync
                def _(sp):
                    def load_parts(qdst, kdst, g, done):
                        rows = PARTS * DH
                        for r in range(PARTS):
                            src = q_scr[g, :, r:r + PARTS, :, :].rearrange("n h s d t -> (n s d) h t")
                            sp.dma_start(qdst[rows * r:rows * (r + 1), :, :], src).then_inc(done, 16)
                            sp.dma_start(kdst[rows * r:rows * (r + 1), :, :],
                                         k_scr[g].rearrange("n h s d t -> (n s d) h t")).then_inc(done, 16)

                    def m_rows(g, u, reg):
                        sp.wait_ge(m_chain, M_STEPS * (g + 1))
                        sp.dma_start(m_scr[reg].rearrange("n p c -> (n p) c"), mT[:]).then_inc(m_stored, 16)
                        sp.wait_ge(m_stored, 16 * (g + 1))
                        src = m_scr[reg].rearrange("n (b c) (s r) -> b (n s) c r", b=4, s=PARTS)
                        for blk in range(4):
                            dst = Qa[M_ROW:M_ROW + PARTS, u, :, :].rearrange(
                                "s h (i b r) -> s b (h i) r", b=4, r=32)[:, blk]
                            sp.dma_start(dst, src[blk]).then_inc(mrow_loaded[u], 16)

                    sp.wait_ge(pads_made, 5)
                    load_parts(Qx[:, 0], Kx[:, 0], bass.ds(0, 1), xop_loaded[0])
                    load_parts(Qx[:, 1], Kx[:, 1], bass.ds(1, 1), xop_loaded[1])
                    load_parts(Qa[:, 0], Ka[:, 0], bass.ds(0, 1), sop_loaded[0])
                    m_rows(0, 0, bass.ds(0, 1))

                    def store_o(n, half):
                        sp.wait_ge(o_read, 2 * n + half + 1 + ONE)
                        sp.dma_start(o_scr[bass.ds(n, 1), :, CHUNK * half:CHUNK * (half + 1)].rearrange(
                            "n p t -> (n p) t"), Os[:, half, :]).then_inc(o_stored[half], 16)

                    def group(n, u, last):
                        if last < 1:
                            sp.wait_ge(mx_read, CPG * (n + 1))
                            load_parts(Qx[:, u], Kx[:, u], bass.ds(n + 2, 1), xop_loaded[u])
                        if last < 2:
                            sp.wait_ge(s_ready, SPG * n + ONE)
                            load_parts(Qa[:, 1 - u], Ka[:, 1 - u], bass.ds(n + 1, 1), sop_loaded[1 - u])
                        store_o(n, 0)
                        if last < 2:
                            m_rows(n + 1, 1 - u, bass.ds(n + 1, 1))
                        store_o(n, 1)

                    with sp.Fori(0, GROUPS // 2 - 1) as i:
                        for u in range(2):
                            group(2 * i + u, u, 0)
                    group(GROUPS - 2, 0, 1)
                    group(GROUPS - 1, 1, 2)
                    for half in range(2):
                        sp.wait_ge(o_stored[half], 16 * GROUPS + ONE)

                @block.gpsimd
                def _(pool):
                    pool.memset(Qx[:], 0.0).then_inc(pads_made, 1)
                    pool.memset(Kx[:], 0.0).then_inc(pads_made, 1)
                    pool.memset(Qa[:], 0.0).then_inc(pads_made, 1)
                    pool.memset(Ka[:], 1.0).then_inc(pads_made, 1)
                    pool.memset(tri[:], 0.0).then_inc(consts_made, 1)
                    pool.wait_ge(consts_made, 5)
                    pool.affine_select(out=tri[:, CHUNK - P:CHUNK], in_=tri[:, CHUNK - P:CHUNK], compare_op=ALU.is_ge,
                                       fill=-BIG, base=0, pattern=[[-1, P]], channel_multiplier=1).then_inc(pads_made, 1)

                    def group(n):
                        for r, k in enumerate(DIAG_UNITS):
                            step = UNITS[k][1][1][3]
                            for hh in range(GH):
                                wait_alone(pool, exp_done, SPG * n + GH * k + hh + 1 + FREE, pads_made)
                                diag = probs[:, k % 2, hh, 0:2 * step].rearrange("p (a c) -> p a c", a=2)[:, :, 0:P]
                                pool.affine_select(out=diag, in_=diag, compare_op=ALU.is_ge, fill=0.0, base=0,
                                                   pattern=[[0, 2], [1, P]], channel_multiplier=-1).then_inc(masked, 1)

                    with pool.Fori(0, GROUPS) as n:
                        group(n)

                @block.scalar
                def _(act):
                    act.sem_inc(exp_done, FREE)

                    def evacuate(n, half):
                        act.wait_ge(pv_done, NU * n + (2 if half == 0 else NU) + 1 + ONE)
                        act.wait_ge(o_stored[half], 16 * n + ONE)
                        act.activation(Os[:, half, :], ps[:, O_BANK, :], ACT.Copy).then_inc(o_read, 1)

                    def group(n):
                        for k, (half, tiles, width) in enumerate(UNITS):
                            act.wait_ge(pv_done, NU * n + k + ONE)
                            for hh in range(GH):
                                e = GH * k + hh
                                act.wait_ge(s_ready, SPG * n + e + 1 + ONE)
                                bank = S_BANK + 2 * (e % 2)
                                act.activation(probs[:, k % 2, hh, 0:width],
                                               ps[:, bank:bank + 2, :].rearrange("p a c -> p (a c)")[:, 0:width],
                                               ACT.Exp, scale=SM_SCALE).then_inc(exp_done, 1)
                                if (k, hh) == (3, 1):
                                    evacuate(n, 0)
                        evacuate(n, 1)

                    with act.Fori(0, GROUPS) as n:
                        group(n)

                @block.tensor
                def _(pe):
                    pe.sem_inc(pv_done, 2)
                    pe.wait_ge(pads_made, 5)

                    def max_chunk(base, f, u, load):
                        i, part, hh, c0, c1 = MAXC[f]
                        if f == 0:
                            pe.wait_ge(xop_loaded[u], load)
                        if not (isinstance(base, int) and base + f < X_SLOTS):
                            pe.wait_ge(mx_read, base + f + 1 - X_SLOTS)
                        pe.matmul(ps[:, X_BANK + f % X_SLOTS, 0:c1 - c0], Qx[:, u, hh, P * i:P * (i + 1)],
                                  Kx[:, u, hh, c0:c1], start=True, stop=True).then_inc(mx_ready, 1)

                    def products(n, u, k):
                        half, tiles, width = UNITS[k]
                        if k == 0:
                            pe.wait_ge(o_read, 2 * n + ONE)
                            pe.wait_ge(v_staged, n + 3)
                        if k == 2:
                            pe.wait_ge(o_read, 2 * n + 1 + ONE)
                        if k in DIAG_UNITS:
                            pe.wait_ge(masked, MPG * n + GH * (DIAG_UNITS.index(k) + 1))
                        else:
                            pe.wait_ge(exp_done, SPG * n + GH * (k + 1) + FREE)
                        for j, q0, w, off in tiles:
                            for hh in range(GH):
                                mm = pe.matmul(ps[32 * hh:32 * hh + VW, O_BANK, q0 - CHUNK * half:q0 - CHUNK * half + w],
                                               Vg[:, u, j, hh, :], probs[:, k % 2, hh, off:off + w],
                                               start=(j == 0), stop=(j == 4 * half + 3), skip_group_check=True)
                        mm.then_inc(pv_done, 1)

                    def scores(n, u, e, load):
                        k, hh = divmod(e, GH)
                        if e == 0:
                            pe.wait_ge(sop_loaded[u], 6 * 16 * load)
                            pe.wait_ge(mrow_loaded[u], 4 * 16 * load)
                        pe.wait_ge(exp_done, SPG * n + e + 1)
                        for j, q0, w, off in UNITS[k][1]:
                            bank = S_BANK + 2 * (e % 2) + off // CHUNK
                            mm = pe.matmul(ps[:, bank, off % CHUNK:off % CHUNK + w], Ka[:, u, hh, P * j:P * (j + 1)],
                                           Qa[:, u, hh, q0:q0 + w], start=True, stop=True)
                        mm.then_inc(s_ready, 1)

                    for f in range(CPG):
                        max_chunk(0, f, 0, 6 * 16)
                    for f in range(AHEAD):
                        max_chunk(CPG, f, 1, 6 * 16)

                    def group(n, u, turn, last):
                        for kind, at in order:
                            if kind == "s":
                                scores(n, u, at, turn + 1)
                                if at % GH == GH - 1 and at >= GH:
                                    products(n, u, at // GH - 1)
                            elif at + AHEAD < CPG and last < 2:
                                max_chunk(CPG * (n + 1), at + AHEAD, 1 - u, 0)
                            elif at + AHEAD >= CPG and last < 1:
                                max_chunk(CPG * (n + 2), at + AHEAD - CPG, u, 6 * 16 * (turn + 2))
                        products(n, u, NU - 1)

                    with pe.Fori(0, GROUPS // 2 - 1) as i:
                        for u in range(2):
                            group(2 * i + u, u, i, 0)
                    group(GROUPS - 2, 0, GROUPS // 2 - 1, 1)
                    group(GROUPS - 1, 1, GROUPS // 2 - 1, 2)

                @block.vector
                def _(dve):
                    dve.memset(ps[:, O_BANK, :], 0.0).then_inc(v_staged, 1)
                    dve.memset(mx[:], -BIG).then_inc(v_staged, 1)
                    dve.tensor_copy(Vg[:, 0, :, :, :], vaug[:, 0, :, :, :]).then_inc(v_staged, 1)
                    dve.wait_ge(v_staged, 3)
                    dve.wait_ge(pads_made, 5)

                    def max_chunk(base, f):
                        i, part, hh, c0, c1 = MAXC[f]
                        w = c1 - c0
                        src = ps[:, X_BANK + f % X_SLOTS, 0:w]
                        if c1 == P * (i + 1):
                            wait_alone(dve, mx_ready, base + f + 1, pads_made)
                        else:
                            dve.wait_ge(mx_ready, base + f + 1)
                        if c1 == P * (i + 1):
                            dve.tensor_tensor_reduce(out=junk[:, f % 4, 0:w], in0=src, in1=tri[:, CHUNK - w:CHUNK], scale=1.0,
                                                     scalar=-BIG, op0=ALU.add, op1=ALU.max,
                                                     accum_out=mx[:, hh, i, 1:2]).then_inc(mx_read, 1)
                        else:
                            dve.tensor_reduce(mx[:, hh, i, 0:1], src, AX.X, ALU.max).then_inc(mx_read, 1)

                    def split_max(g):
                        c = M_STEPS * g
                        dve.wait_ge(mx_read, CPG * (g + 1))
                        dve.tensor_tensor(mm_[:].rearrange("p (h i) -> p h i", h=GH), mx[:, :, :, 0], mx[:, :, :, 1],
                                          ALU.max).then_inc(m_chain, 1)
                        dve.wait_ge(m_chain, c + 1)
                        dve.tensor_scalar(msp[:, 0:32], mm_[:], -1.0, None, ALU.mult).then_inc(m_chain, 1)
                        dve.wait_ge(m_chain, c + 2)
                        dve.scalar_tensor_tensor(out=mr[:], in0=mm_[:], scalar=-1.0, in1=msp[:, 0:32], op0=ALU.mult,
                                                 op1=ALU.subtract).then_inc(m_chain, 1)
                        dve.wait_ge(m_chain, c + 3)
                        dve.tensor_copy(msp[:, 32:64], mr[:]).then_inc(m_chain, 1)
                        dve.wait_ge(m_chain, c + 4)
                        dve.tensor_tensor(msp[:, 64:96], mr[:], msp[:, 32:64], ALU.subtract).then_inc(m_chain, 1)
                        dve.wait_ge(m_chain, c + 5)
                        dve.wait_ge(m_stored, 16 * g)
                        dve.transpose(mT[:], msp[:]).then_inc(m_chain, 1)

                    for f in range(CPG):
                        max_chunk(0, f)
                    split_max(0)
                    for f in range(AHEAD):
                        max_chunk(CPG, f)

                    def group(n, u, last):
                        for f in range(CPG):
                            if f == 12 and last < 2:
                                dve.wait_ge(pv_done, NU * n + 1 + ONE)
                                dve.tensor_copy(Vg[:, 1 - u, :, :, :], vaug[:, bass.ds(n + 1, 1), :, :, :].rearrange(
                                    "p n j h d -> p (n j) h d")).then_inc(v_staged, 1)
                            if f + AHEAD < CPG and last < 2:
                                max_chunk(CPG * (n + 1), f + AHEAD)
                            elif f + AHEAD >= CPG and last < 1:
                                max_chunk(CPG * (n + 2), f + AHEAD - CPG)
                            if f + AHEAD == CPG - 1 and last < 2:
                                split_max(n + 1)

                    with dve.Fori(0, GROUPS // 2 - 1) as i:
                        for u in range(2):
                            group(2 * i + u, u, 0)
                    group(GROUPS - 2, 0, 1)
                    group(GROUPS - 1, 1, 2)

        with ExitStack() as phase:
            def sa(name, shape, dt=F32):
                return phase.enter_context(nc.sbuf_tensor(name, shape, dt))

            ot = sa("ot", [P, HG, CHUNK])
            xc = sa("xc", [P, TPC, D])
            xb = sa("xb", [P, TPC, D])
            rden = sa("rden", [P, 2, HEADS])
            attn = sa("attn", [P, 2, D])
            attnT = sa("attnT", [P, 2, P])
            z = sa("z", [P, TPC, D])
            stats = sa("stats", [P, 2, TPC, 6])
            mv = sa("mv", [P, 2, TPC, 2])
            veps = sa("veps", [P, 2, TPC])
            rstd = sa("rstd", [P, 2, TPC])
            x1 = sa("x1", [P, TPC, D])
            x1b = sa("x1b", [P, TPC, D])
            x1T = sa("x1T", [P, CHUNK])
            gate = sa("gate", [P, FC, CHUNK])
            upv = sa("upv", [P, FC, CHUNK])
            h = sa("h", [P, FC, CHUNK])
            sG = sa("sG", [P, FC, CHUNK])
            sim = sa("sim", [P, TPC, 2 * RH * NK])
            V = sa("V", [P, TPC, 2 * RH, KPH])
            ixu = sa("ixu", [P, TPC, RH, KPH], U32)
            ixf = sa("ixf", [P, TPC, RH * KPH])
            ymark = sa("ymark", [P, TPC, RH, NK])
            cand = sa("cand", [P, TPC, RH, KPH, KPH])
            cmark = sa("cmark", [P, TPC, RH, KPH, KPH])
            T = sa("T", [P, TPC, RH, KPH])
            EX, EY, EC = 0, RH * XIN, RH * XIN + RH * NK
            shift = sa("shift", [P, TPC, EC + RH * NK])
            edge_ab = sa("edge_ab", [P, RH, KPH, KPH])
            edge_a = sa("edge_a", [P, RH * KPH])
            edge_ax = sa("edge_ax", [P, RH * KPH, XIN])
            edge_x = sa("edge_x", [P, TPC, RH, XIN])
            picked = sa("picked", [P, RH * KPH, KPH])
            sum_a = sa("sum_a", [P, RH, KPH])
            den = sa("den", [P, RH])
            rz = sa("rz", [P, RH])
            far = sa("far", [P, RH, KPH])
            rest = sa("rest", [P, TPC, RH])
            exn = sa("exn", [P, TPC, RH, XIN])
            eym = sa("eym", [P, TPC, RH, NK])
            A = sa("A", [P, 2, RH, XIN, NK])
            E = sa("E", [P, 2, RH, XIN, NK])
            Wt = sa("Wt", [P, 2, FC, P])
            z2 = sa("z2", [P, TPC, D])
            fin = sa("fin", [P, TPC, D])

            ATTN, ATTNT, Y, X1T, RING, SIM, AT, OUT = 0, 1, (3, 4), 1, (3, 4), (5, 2), 6, 7
            PE_ORDER = ["sim2", "sim3", "front0'", "ffn0", "front1'", "ffn1", "AT0", "front2'", "front3'", "AT1",
                        "out0", "front4'", "out1", "front5'", "AT2", "x1T'", "sim0'", "sim1'", "out2", "AT3", "out3"]
            DVE_ORDER = ["r2_0", "r2_1", "front0'", "r1_2", "front1'", "dense0", "r2_2", "front2'", "wt0", "r1_3",
                         "front3'", "dense1", "r2_3", "front4'", "wt1", "z2_0", "front5'", "dense2", "z2_1", "x1'",
                         "wt2", "dense3", "r1_0'", "z2_2", "wt3", "r1_1'", "z2_3", "fin"]
            POOL_ORDER = ["xb'", "spread0", "shift2", "spread1", "h", "shift3", "spread2", "pow'", "spread3",
                          "shift0'", "shift1'", "pow2", "x1b'"]
            ACT_ORDER = ["sim2", "sim3", "ffn0", "turned0'", "ffn1", "exps2", "turned1'", "turned2'", "exps3",
                         "turned3'", "x1T'", "sim0'", "sim1'", "exps0'", "exps1'"]

            def run(order, table, c, more=True, only=False):
                for name in order:
                    later = name.endswith("'")
                    if (only and not later) or (later and not (more or only)):
                        continue
                    what = name.rstrip("'")
                    at = c if only or not later else c + 1
                    key = what.rstrip("0123456789") if what not in table else what
                    if key in table and what in table:
                        table[what](at)
                    else:
                        table[key](at, int(what[len(key):]))

            with nc.Block() as block:
                @block.sync
                def _(sp):
                    def load(b, u):
                        c = 2 * b + u
                        sp.wait_ge(oT_ready, TPC * c + ONE)
                        sp.dma_start(ot[:], o_scr[bass.ds(b * HG, HG), :, CHUNK * u:CHUNK * (u + 1)].rearrange(
                            "g p t -> p g t")).then_inc(ot_loaded, 16)
                        sp.wait_ge(xb_ready, c + ONE)
                        sp.dma_start(xc[:], x_chunks[bass.ds(c, 1)].rearrange(
                            "c p t d -> (c p) t d")).then_inc(xc_loaded, 16)

                    def store(c):
                        sp.wait_ge(fin_ready, c + 1)
                        sp.dma_start(out_chunks[bass.ds(c, 1)].rearrange("c p t d -> (c p) t d"),
                                     fin[:]).then_inc(out_stored, 16)

                    load(0, 0)
                    with sp.Fori(0, BATCH - 1) as b:
                        load(b, 1)
                        store(2 * b)
                        load(b + 1, 0)
                        store(2 * b + 1)
                    load(BATCH - 1, 1)
                    store(CHUNKS - 2)
                    store(CHUNKS - 1)
                    sp.wait_ge(out_stored, 16 * CHUNKS + ONE)

                @block.gpsimd
                def _(pool):
                    def residual(c):
                        pool.wait_ge(xc_loaded, 16 * c + 16)
                        pool.wait_ge(z_done, TPC * c + ONE)
                        pool.tensor_tensor(xb[:], xc[:], bo_row[:].unsqueeze(1).broadcast_to([P, TPC, D]),
                                           ALU.add).then_inc(xb_ready, 1)

                    def power(c):
                        pool.wait_ge(var_ready, c + 1)
                        pool.tensor_tensor(rstd[:, 0, :], veps[:, 0, :], mhalf[:], ALU.pow).then_inc(rstd_ready, 1)

                    def power2(c):
                        pool.wait_ge(var2_ready, c + 1)
                        pool.tensor_tensor(rstd[:, 1, :], veps[:, 1, :], mhalf[:], ALU.pow).then_inc(rstd2_ready, 1)

                    def residual2(c):
                        pool.wait_ge(x1_ready, c + 1)
                        pool.wait_ge(z2_done, TPC * c + ONE)
                        pool.tensor_tensor(x1b[:], x1[:], bd_row[:].unsqueeze(1).broadcast_to([P, TPC, D]),
                                           ALU.add).then_inc(x1b_ready, 1)

                    def below_max(c, t):
                        pool.wait_ge(cand_ready, TPC * c + t + 1)
                        pool.tensor_tensor(shift[:, t, EX:EY].rearrange("p (h x) -> p h x", h=RH),
                                           sim[:, t, 0:RH * NK].rearrange("p (h x) -> p h x", h=RH)[:, :, 0:XIN],
                                           V[:, t, 0:RH, 0:1].broadcast_to([P, RH, XIN]), ALU.subtract)
                        pool.tensor_tensor(shift[:, t, EY:EC].rearrange("p (h y) -> p h y", h=RH),
                                           sim[:, t, RH * NK:].rearrange("p (h y) -> p h y", h=RH),
                                           V[:, t, RH:2 * RH, 0:1].broadcast_to([P, RH, NK]), ALU.subtract)
                        pool.tensor_tensor(shift[:, t, EC:].rearrange("p (h y) -> p h y", h=RH),
                                           cand[:, t].rearrange("p h a b -> p h (a b)"),
                                           T[:, t, :, 0:1].broadcast_to([P, RH, NK]), ALU.subtract).then_inc(shifted, 1)

                    def spread(c, t):
                        m, s = TPC * c + t, t % 2
                        pool.wait_ge(edge_ready, m + 1)
                        pool.wait_ge(AT_ready, m + 1)
                        pool.tensor_tensor(A[:, s], sim[:, t, RH * NK:].rearrange("p (h o y) -> p h o y", h=RH, o=1)
                                           .broadcast_to([P, RH, XIN, NK]),
                                           edge_x[:, t].unsqueeze(3).broadcast_to([P, RH, XIN, NK]), ALU.subtract)
                        pool.tensor_tensor(E[:, s], eym[:, t].unsqueeze(2).broadcast_to([P, RH, XIN, NK]),
                                           exn[:, t].unsqueeze(3).broadcast_to([P, RH, XIN, NK]),
                                           ALU.mult).then_inc(de_ready, 1)

                    def hidden(c):
                        for f in range(FC):
                            pool.wait_ge(ffn_read, 3 * FC * c + 2 * f + 2 + FREE)
                            pool.wait_ge(out_ready, TPC * c + ONE)
                            pool.tensor_tensor(h[:, f, :], gate[:, f, :], upv[:, f, :], ALU.mult).then_inc(h_ready, 1)

                    steps = {"xb": residual, "pow": power, "pow2": power2, "x1b": residual2, "shift": below_max,
                             "spread": spread, "h": hidden}
                    run(POOL_ORDER, steps, 0, only=True)
                    with pool.Fori(0, CHUNKS - 1) as c:
                        run(POOL_ORDER, steps, c)
                    run(POOL_ORDER, steps, CHUNKS - 1, more=False)

                @block.scalar
                def _(act):
                    act.sem_inc(ffn_read, FREE)

                    def turned(c, t):
                        act.wait_ge(attnT_ready, TPC * c + t + 1)
                        if t >= 2:
                            act.wait_ge(y_ready, TPC * c + t - 1)
                        act.activation(attnT[:, t % 2, :], ps[:, ATTNT, 0:P], ACT.Copy).then_inc(attnT_copied, 1)

                    def x1_turned(c):
                        act.wait_ge(x1T_ready, c + 1)
                        act.activation(x1T[:], ps[:, X1T, :], ACT.Copy).then_inc(x1T_copied, 1)

                    def copy_sim(c, t):
                        act.wait_ge(sim_ready, TPC * c + t + 1)
                        if t < 2 and not isinstance(c, int):
                            act.wait_ge(de_ready, TPC * c + t + 1 - TPC)
                        act.activation(sim[:, t, :], ps[:, SIM[t % 2], :], ACT.Copy).then_inc(sim_copied, 1)

                    def ffn(c, part):
                        for k in range(6 * part, 6 * part + 6):
                            act.wait_ge(ffn_ready, 3 * FC * c + k + 1)
                            src = ps[:, RING[k % 2], :]
                            if k < 2 * FC:
                                f = k // 2
                                if k < 2:
                                    act.wait_ge(h_ready, FC * c + ONE)
                                act.activation((gate if k % 2 == 0 else upv)[:, f, :], src,
                                               ACT.Silu if k % 2 == 0 else ACT.Identity,
                                               bias=bgu[:, k % 2, f:f + 1]).then_inc(ffn_read, 1)
                            else:
                                act.wait_ge(Wt_ready, TPC * c + ONE)
                                act.activation(sG[:, k - 2 * FC, :], src, ACT.Silu).then_inc(ffn_read, 1)

                    def exps(c, t):
                        act.wait_ge(shifted, TPC * c + t + 1)
                        act.activation(shift[:, t, :], shift[:, t, :], ACT.Exp).then_inc(exps_ready, 1)

                    steps = {"turned": turned, "x1T": x1_turned, "sim": copy_sim, "ffn": ffn, "exps": exps}
                    run(ACT_ORDER, steps, 0, only=True)
                    with act.Fori(0, CHUNKS - 1) as c:
                        run(ACT_ORDER, steps, c)
                    run(ACT_ORDER, steps, CHUNKS - 1, more=False)

                @block.tensor
                def _(pe):
                    def front(c, step):
                        if step == 0:
                            pe.wait_ge(ot_loaded, 16 * c + 16)
                        if step < TPC:
                            pe.wait_ge(attn_ready, TPC * c + step + ONE)
                            for g in range(HG):
                                mm = pe.transpose(ps[:, ATTN, P * g:P * (g + 1)], ot[:, g, P * step:P * (step + 1)], ident[:])
                            mm.then_inc(oT_ready, 1)
                        t = step - 1
                        if 0 <= t < TPC:
                            pe.wait_ge(attn_ready, TPC * c + t + 1 + ONE)
                            if t > 0:
                                pe.wait_ge(attnT_copied, TPC * c + t)
                            pe.transpose(ps[:, ATTNT, 0:P], attn[:, t % 2, :], ident[:]).then_inc(attnT_ready, 1)
                        t = step - 2
                        if 0 <= t < TPC:
                            pe.wait_ge(attnT_copied, TPC * c + t + 1)
                            if t < 2:
                                pe.wait_ge(ffn_read, 3 * FC * c + FREE)
                            else:
                                pe.wait_ge(z_done, TPC * c + t - 1 + ONE)
                            pe.matmul(ps[:, Y[t % 2], 0:P], attnT[:, t % 2, :], WoT[:],
                                      start=True, stop=True).then_inc(y_ready, 1)

                    def x1_turn(c):
                        pe.wait_ge(x1_ready, c + 1)
                        pe.wait_ge(attnT_copied, TPC * c + TPC)
                        for t in range(TPC):
                            mm = pe.transpose(ps[:, X1T, P * t:P * (t + 1)], x1[:, t, :], ident[:])
                        mm.then_inc(x1T_ready, 1)

                    def sims(c, t):
                        if t == 0:
                            pe.wait_ge(x1T_copied, c + 1)
                        if not (isinstance(c, int) and TPC * c + t < 2):
                            pe.wait_ge(sim_copied, TPC * c + t - 1 + ONE)
                        pe.matmul(ps[:, SIM[t % 2], :], x1T[:, P * t:P * (t + 1)],
                                  Wsim[:].rearrange("p a b -> p (a b)"), start=True, stop=True).then_inc(sim_ready, 1)

                    def ffn(c, part):
                        for k in range(6 * part, 6 * part + 6):
                            pe.wait_ge(ffn_read, 3 * FC * c + k + 1)
                            if k < 2 * FC:
                                w = (Wg_sb if k % 2 == 0 else Wu_sb)[:, P * (k // 2):P * (k // 2 + 1)]
                            else:
                                w = downT[:, P * (k - 2 * FC):P * (k - 2 * FC + 1)]
                            pe.matmul(ps[:, RING[k % 2], :], w, x1T[:], start=True, stop=True).then_inc(ffn_ready, 1)

                    def combine(c, t):
                        m, s = TPC * c + t, t % 2
                        pe.wait_ge(A_ready, m + 1)
                        pe.wait_ge(Wt_ready, m + ONE)
                        Af = A[:, s].rearrange("p h x y -> p h (x y)")
                        for e in range(FC):
                            for hd in range(RH):
                                mm = pe.matmul(ps[:, AT, P * e:P * (e + 1)], Af[:, hd, P * e:P * (e + 1)], ident[:],
                                               start=(hd == 0), stop=(hd == RH - 1))
                        mm.then_inc(AT_ready, 1)

                    def output(c, t):
                        m, s = TPC * c + t, t % 2
                        dst = ps[:, OUT, 0:P]
                        pe.wait_ge(h_ready, FC * c + FC + ONE)
                        pe.wait_ge(z2_done, m + ONE)
                        for f in range(FC):
                            pe.matmul(dst, h[:, f, P * t:P * (t + 1)], Wd_sb[:, f, :], start=(f == 0), stop=False)
                        pe.wait_ge(Wt_ready, m + 1 + ONE)
                        for e in range(FC):
                            mm = pe.matmul(dst, Wt[:, s, e, :], up_sb[:, e, :], start=False, stop=(e == FC - 1))
                        mm.then_inc(out_ready, 1)

                    pe.sem_inc(AT_ready, FREE)
                    steps = {"front": front, "x1T": x1_turn, "sim": sims, "ffn": ffn, "AT": combine, "out": output}
                    run(PE_ORDER, steps, 0, only=True)
                    with pe.Fori(0, CHUNKS - 1) as c:
                        run(PE_ORDER, steps, c)
                    run(PE_ORDER, steps, CHUNKS - 1, more=False)

                @block.vector
                def _(dve):
                    linked = {"now": 0, "before": 0}

                    def link(ins, alone=False):
                        linked["now"] += 1
                        ins.then_inc(c_chain, 1)
                        value = linked["before"] + linked["now"]
                        if alone:
                            wait_alone(dve, c_chain, value, consts_made)
                        else:
                            dve.wait_ge(c_chain, value)

                    def r1(c, t):
                        m = TPC * c + t
                        wait_alone(dve, sim_copied, m + 1 + ONE, consts_made)
                        for g in range(2 * RH):
                            last = dve.max(V[:, t, g, :], sim[:, t, NK * g:NK * (g + 1)])
                        link(last, alone=True)
                        for hd in range(RH):
                            dve.max_index(ixu[:, t, hd, :], V[:, t, hd, :], sim[:, t, NK * hd:NK * (hd + 1)])
                        for hd in range(RH):
                            dve.match_replace(ymark[:, t, hd, :], V[:, t, RH + hd, :],
                                              sim[:, t, NK * (RH + hd):NK * (RH + hd + 1)], BIG)
                        link(dve.tensor_tensor(cand[:, t], V[:, t, 0:RH, :].unsqueeze(3).broadcast_to([P, RH, KPH, KPH]),
                                               V[:, t, RH:2 * RH, :].unsqueeze(2).broadcast_to([P, RH, KPH, KPH]),
                                               ALU.add), alone=True)
                        for hd in range(RH):
                            last = dve.max(T[:, t, hd, :], cand[:, t, hd].rearrange("p a b -> p (a b)"))
                        last.then_inc(cand_ready, 1)
                        wait_alone(dve, cand_ready, m + 1, consts_made)
                        for hd in range(RH):
                            dve.match_replace(cmark[:, t, hd].rearrange("p a b -> p (a b)"), T[:, t, hd, :],
                                              cand[:, t, hd].rearrange("p a b -> p (a b)"), BIG)
                        link(dve.tensor_copy(ixf[:, t, :], ixu[:, t].rearrange("p h a -> p (h a)")), alone=True)

                    def r2(c, t):
                        m = TPC * c + t
                        dve.tensor_scalar(edge_ab[:], cmark[:, t], MARKED, FAR, ALU.is_lt, ALU.mult)
                        link(dve.tensor_tensor(edge_ax[:], ixf[:, t, :].unsqueeze(2).broadcast_to([P, RH * KPH, XIN]),
                                               iota8[:].unsqueeze(1).broadcast_to([P, RH * KPH, XIN]),
                                               ALU.not_equal))
                        link(dve.tensor_tensor(edge_ab[:], edge_ab[:],
                                               V[:, t, RH:2 * RH, :].unsqueeze(2).broadcast_to([P, RH, KPH, KPH]),
                                               ALU.add))
                        dve.tensor_reduce(edge_a[:], edge_ab[:].rearrange("p h a b -> p (h a) b"), AX.X, ALU.min)
                        dve.wait_ge(exps_ready, m + 1)
                        link(dve.scalar_tensor_tensor(out=picked[:], in0=cmark[:, t].rearrange("p h a b -> p (h a) b"),
                                                      scalar=MARKED,
                                                      in1=shift[:, t, EC:].rearrange("p (a b) -> p a b", b=KPH),
                                                      op0=ALU.is_ge, op1=ALU.mult))
                        dve.tensor_reduce(sum_a[:].rearrange("p h a -> p (h a)"), picked[:], AX.X, ALU.add)
                        link(dve.scalar_tensor_tensor(out=edge_ax[:], in0=edge_ax[:], scalar=FAR,
                                                      in1=edge_a[:].unsqueeze(2).broadcast_to([P, RH * KPH, XIN]),
                                                      op0=ALU.mult, op1=ALU.add))
                        dve.tensor_reduce(den[:], sum_a[:], AX.X, ALU.add)
                        link(dve.scalar_tensor_tensor(out=far[:].rearrange("p h a -> p (h a)"), in0=ixf[:, t, :],
                                                      scalar=float(XIN), in1=sum_a[:].rearrange("p h a -> p (h a)"),
                                                      op0=ALU.is_ge, op1=ALU.mult))
                        dve.reciprocal(rz[:], den[:])
                        dve.tensor_reduce(rest[:, t, :], far[:], AX.X, ALU.add)
                        link(dve.tensor_reduce(edge_x[:, t], edge_ax[:].rearrange("p (h a) x -> p h x a", h=RH), AX.X,
                                               ALU.min))
                        dve.tensor_tensor(rest[:, t, :], rest[:, t, :], rz[:], ALU.mult)
                        dve.tensor_tensor(exn[:, t], shift[:, t, EX:EY].rearrange("p (h x) -> p h x", h=RH),
                                          rz[:].unsqueeze(2).broadcast_to([P, RH, XIN]), ALU.mult)
                        dve.scalar_tensor_tensor(out=eym[:, t].rearrange("p h y -> p (h y)"),
                                                 in0=ymark[:, t].rearrange("p h y -> p (h y)"), scalar=MARKED,
                                                 in1=shift[:, t, EY:EC], op0=ALU.is_ge, op1=ALU.mult).then_inc(edge_ready, 1)

                    def dense(c, t):
                        m, s = TPC * c + t, t % 2
                        dve.wait_ge(de_ready, m + 1)
                        flat = A[:, s].rearrange("p h x y -> p (h x y)")
                        link(dve.scalar_tensor_tensor(out=flat, in0=flat, scalar=0.0,
                                                      in1=E[:, s].rearrange("p h x y -> p (h x y)"),
                                                      op0=ALU.is_ge, op1=ALU.mult))
                        end = A[:, s, :, XIN - 1, NK - 1]
                        dve.tensor_tensor(end, end, rest[:, t, :], ALU.add).then_inc(A_ready, 1)

                    def wt(c, t):
                        m, s = TPC * c + t, t % 2
                        dve.wait_ge(AT_ready, m + 1 + FREE)
                        if t == 0:
                            dve.wait_ge(ffn_read, 3 * FC * (c + 1) + FREE)
                        if t >= 2:
                            dve.wait_ge(out_ready, m - 1 + ONE)
                        dve.tensor_tensor(Wt[:, s], ps[:, AT, :].rearrange("p (e t) -> p e t", e=FC),
                                          sG[:, :, P * t:P * (t + 1)], ALU.mult).then_inc(Wt_ready, 1)

                    def moments(which, src, t, done):
                        link(dve.bn_stats(stats[:, which, t, :], src[:, t, :]), alone=True)
                        dve.bn_aggr(mv[:, which, t, :], stats[:, which, t, :]).then_inc(done, 1)

                    def front(c, step):
                        if step < TPC:
                            s = step % 2
                            dve.wait_ge(oT_ready, TPC * c + step + 1 + ONE)
                            src = ps[:, ATTN, :].rearrange("p (h r) -> p h r", r=32)
                            link(dve.reciprocal(rden[:, s, :], src[:, :, DH]))
                            dve.tensor_tensor(attn[:, s, :].rearrange("p (h d) -> p h d", d=DH), src[:, :, 0:DH],
                                              rden[:, s, :].unsqueeze(2).broadcast_to([P, HEADS, DH]),
                                              ALU.mult).then_inc(attn_ready, 1)
                        t = step - 2
                        if 0 <= t < TPC:
                            dve.wait_ge(y_ready, TPC * c + t + 1)
                            dve.wait_ge(xb_ready, c + 1 + ONE)
                            dve.tensor_tensor(z[:, t, :], ps[:, Y[t % 2], 0:P], xb[:, t, :], ALU.add).then_inc(z_done, 1)
                            dve.wait_ge(z_done, TPC * c + t + 1 + ONE)
                            moments(0, z, t, mv_done)
                        if step == TPC + 1:
                            dve.wait_ge(mv_done, TPC * c + TPC)
                            dve.tensor_scalar(veps[:, 0, :], mv[:, 0, :, 1], EPS, None, ALU.add).then_inc(var_ready, 1)

                    def normalise(c):
                        dve.wait_ge(rstd_ready, c + 1)
                        if not isinstance(c, int):
                            dve.wait_ge(x1b_ready, c)
                        for t in range(TPC):
                            last = dve.tensor_scalar(x1[:, t, :], z[:, t, :], mv[:, 0, t, 0:1], rstd[:, 0, t:t + 1],
                                                     ALU.subtract, ALU.mult)
                        last.then_inc(x1_ready, 1)

                    def last_sum(c, t):
                        m = TPC * c + t
                        dve.wait_ge(out_ready, m + 1 + ONE)
                        dve.wait_ge(x1b_ready, c + 1)
                        dve.tensor_tensor(z2[:, t, :], ps[:, OUT, 0:P], x1b[:, t, :], ALU.add).then_inc(z2_done, 1)
                        dve.wait_ge(z2_done, m + 1 + ONE)
                        moments(1, z2, t, mv2_done)

                    def finish(c):
                        dve.wait_ge(mv2_done, TPC * (c + 1))
                        dve.tensor_scalar(veps[:, 1, :], mv[:, 1, :, 1], EPS, None, ALU.add).then_inc(var2_ready, 1)
                        dve.wait_ge(rstd2_ready, c + 1)
                        dve.wait_ge(out_stored, 16 * c + ONE)
                        for t in range(TPC):
                            last = dve.tensor_scalar(fin[:, t, :], z2[:, t, :], mv[:, 1, t, 0:1], rstd[:, 1, t:t + 1],
                                                     ALU.subtract, ALU.mult)
                        last.then_inc(fin_ready, 1)

                    steps = {"front": front, "x1": normalise, "r1_": r1, "r2_": r2, "dense": dense, "wt": wt,
                             "z2_": last_sum, "fin": finish}
                    run(DVE_ORDER, steps, 0, only=True)
                    first = linked["now"]
                    with dve.Fori(0, CHUNKS - 1) as c:
                        linked.update(now=0, before=first + LINKS * c)
                        run(DVE_ORDER, steps, c)
                        assert linked["now"] == LINKS, linked["now"]
                    linked.update(now=0, before=first + LINKS * (CHUNKS - 1))
                    run(DVE_ORDER, steps, CHUNKS - 1, more=False)


_INS = ["L0_attn_x", "L0_attn_W_qkv", "L0_attn_b_qkv", "L0_attn_W_o", "L0_attn_b_o", "L0_ffn_Wg", "L0_ffn_bg",
        "L0_ffn_Wu", "L0_ffn_bu", "L0_ffn_Wd", "L0_ffn_bd", "L0_ffn_Wq", "L0_ffn_keys", "L0_ffn_down_embed",
        "L0_ffn_up_embed"]
_OUTS = [((4, 1024, 128), "float32")]


def kernel(**inputs):
    import numpy as _np
    import concourse.bacc as _bacc
    from concourse import mybir as _mybir
    from concourse.bass_utils import run_bass_kernel_spmd as _run

    nc = _bacc.Bacc("TRN2", target_bir_lowering=False, num_devices=1)
    arrays, args = {}, []
    for name in _INS:
        a = _np.ascontiguousarray(inputs[name])
        arrays[f"in_{name}_dram"] = a
        args.append(nc.dram_tensor(f"in_{name}_dram", a.shape, _mybir.dt.from_np(a.dtype), kind="ExternalInput").ap())
    for i, (shape, dtype) in enumerate(_OUTS):
        dt = _mybir.dt.from_np(_np.dtype(dtype))
        args.append(nc.dram_tensor(f"out_{i}_dram", shape, dt, kind="ExternalOutput").ap())
    build(nc, *args)
    r = _run(nc, [arrays], core_ids=[0])
    got = tuple(r.results[0][f"out_{i}_dram"] for i in range(len(_OUTS)))
    return got[0]
```

```python
from contextlib import ExitStack

import concourse.bass as bass
from concourse import mybir

F32 = mybir.dt.float32
BF16 = mybir.dt.bfloat16
U32 = mybir.dt.uint32
ALU = mybir.AluOpType
ACT = mybir.ActivationFunctionType
AX = mybir.AxisListType

P = 128
BATCH, SEQ, D = 4, 1024, 128
HEADS, DH = 16, 8
TOKENS = BATCH * SEQ
TILES = TOKENS // P
CHUNK = 512
CHUNKS = TOKENS // CHUNK
TPC = CHUNK // P
HG = 4
GH = HEADS // HG
GROUPS = BATCH * HG
PARTS = 3
SPLIT_ROWS = PARTS * PARTS * DH
M_ROW = SPLIT_ROWS
VW = DH + 1
F = 512
FC = F // P
NEXP = 512
NK = 64
RH = 4
KPH = 8
XIN = NEXP // NK
EPS = 1e-5
SM_SCALE = float(DH) ** -0.5
BIG = 3.0e38
MARKED = 2.9e38
FAR = 1.0e38

UNITS = []
for _half, _tiles in ((0, (0, 1)), (0, (2, 3)), (1, (0, 1)), (1, (2, 3)), (1, (4, 5)), (1, (6, 7))):
    _at, _off = [], 0
    for _j in _tiles:
        _q0 = max(P * _j, CHUNK * _half)
        _w = CHUNK * (_half + 1) - _q0
        _at.append((_j, _q0, _w, _off))
        _off += _w
    UNITS.append((_half, _at, _off))
NU = len(UNITS)
PIECES = [(_k, _a) for _k in range(NU) for _a in range(2)]
PPG = len(PIECES)
HALF_PIECES = sum(2 for _half, _at, _w in UNITS if _half == 0)
DIAG_UNITS = [k for k, (h, at, w) in enumerate(UNITS) if at[0][0] >= 4 * h]
SPG = NU * GH
MPG = len(DIAG_UNITS) * GH

MAXC = []
for _i in range(SEQ // P - 1, -1, -1):
    _end = P * (_i + 1)
    for _part, (_c0, _c1) in enumerate([(0, CHUNK), (CHUNK, _end)] if _end > CHUNK else [(0, _end)]):
        for _hh in range(GH):
            MAXC.append((_i, _part, _hh, _c0, _c1))
CPG = len(MAXC)
AHEAD = 20
GROUP_ORDER = "psxxxpxxsxxsxsxpxspxxsxxpxxxspxxssxxsxpxsxxxsxpxxxsxspsxxsxpxxsxsxxsxpxxsxpxsxsxsxsx"
CARRIED = 4
COPY_AT = (12, 4)
X_SLOTS = 3
FREE = 2
ONE = 1
S_BANK, O_BANK, X_BANK = 0, 4, 5
PV_START = 4
M_STEPS = 6
LINKS = 34


def wait_alone(eng, signal, value, done):
    if not isinstance(value, int):
        value = eng.to_reg(value)
    eng.wait_ge(done, 1)
    eng.wait_ge(signal, value)


def build(nc, x, W_qkv, b_qkv, W_o, b_o, Wg, bg, Wu, bu, Wd, bd, Wq, keys, down, up, out):
    q_scr = nc.dram_tensor("q_scr", [GROUPS, GH, 5, DH, SEQ], BF16).ap()
    k_scr = nc.dram_tensor("k_scr", [GROUPS, GH, PARTS, DH, SEQ], BF16).ap()
    m_scr = nc.dram_tensor("m_scr", [GROUPS, P, PARTS * 32], BF16).ap()
    o_scr = nc.dram_tensor("o_scr", [GROUPS, P, SEQ], F32).ap()

    with ExitStack() as ctx:
        def sb(name, shape, dt=F32):
            return ctx.enter_context(nc.sbuf_tensor(name, shape, dt))

        def sem(name):
            return ctx.enter_context(nc.semaphore(name))

        ps = ctx.enter_context(nc.psum_tensor("ps", [P, 8, 512], F32))

        ident = sb("ident", [P, P])
        WqkvT = sb("WqkvT", [P, 3, P])
        WoT = sb("WoT", [P, P])
        downT = sb("downT", [P, NEXP])
        Wsim = sb("Wsim", [P, 4, P])
        Wg_sb = sb("Wg_sb", [P, F])
        Wu_sb = sb("Wu_sb", [P, F])
        Wd_sb = sb("Wd_sb", [P, FC, D])
        up_sb = sb("up_sb", [P, FC, D])
        bqk = sb("bqk", [P, 2])
        bgu = sb("bgu", [P, 2, FC])
        bv_row = sb("bv_row", [P, D])
        bo_row = sb("bo_row", [P, D])
        bd_row = sb("bd_row", [P, D])
        iota8 = sb("iota8", [P, XIN])
        mhalf = sb("mhalf", [P, TPC])

        x_loaded = [sem(f"x_loaded{u}") for u in range(2)]
        wqkv_loaded = sem("wqkv_loaded")
        prep_loaded = sem("prep_loaded")
        wts_loaded = sem("wts_loaded")
        kbd_zeroed = sem("kbd_zeroed")
        consts_made = sem("consts_made")
        wT_ready = sem("wT_ready")
        wT_read = sem("wT_read")
        xT_ready = sem("xT_ready")
        xT_read = sem("xT_read")
        qk_ready = sem("qk_ready")
        v_ready = sem("v_ready")
        q_read = sem("q_read")
        v_read = sem("v_read")
        r_made = sem("r_made")
        p2_made = sem("p2_made")
        p3_made = sem("p3_made")
        qk_stored = [sem(f"qk_stored{u}") for u in range(2)]
        p3_stored = [sem(f"p3_stored{u}") for u in range(2)]
        pads_made = sem("pads_made")
        xop_loaded = [sem(f"xop_loaded{u}") for u in range(2)]
        sop_loaded = [sem(f"sop_loaded{u}") for u in range(2)]
        mrow_loaded = [sem(f"mrow_loaded{u}") for u in range(2)]
        mx_ready = sem("mx_ready")
        mx_read = sem("mx_read")
        m_chain = sem("m_chain")
        m_stored = sem("m_stored")
        v_staged = sem("v_staged")
        s_ready = sem("s_ready")
        exp_done = sem("exp_done")
        masked = sem("masked")
        pv_done = sem("pv_done")
        o_read = sem("o_read")
        o_stored = [sem(f"o_stored{h}") for h in range(2)]
        ot_loaded = sem("ot_loaded")
        oT_ready = sem("oT_ready")
        attn_ready = sem("attn_ready")
        attnT_ready = sem("attnT_ready")
        attnT_copied = sem("attnT_copied")
        y_ready = sem("y_ready")
        xb_ready = sem("xb_ready")
        z_done = sem("z_done")
        var_ready = sem("var_ready")
        rstd_ready = sem("rstd_ready")
        x1_ready = sem("x1_ready")
        x1T_ready = sem("x1T_ready")
        x1T_copied = sem("x1T_copied")
        ffn_ready = sem("ffn_ready")
        ffn_read = sem("ffn_read")
        h_ready = sem("h_ready")
        sim_ready = sem("sim_ready")
        sim_copied = sem("sim_copied")
        route_done = sem("route_done")
        cand_ready = sem("cand_ready")
        shifted = sem("shifted")
        exps_ready = sem("exps_ready")
        edge_ready = sem("edge_ready")
        de_ready = sem("de_ready")
        A_ready = sem("A_ready")
        AT_ready = sem("AT_ready")
        Wt_ready = sem("Wt_ready")
        out_ready = sem("out_ready")
        x1b_ready = sem("x1b_ready")
        z2_done = sem("z2_done")
        var2_ready = sem("var2_ready")
        rstd2_ready = sem("rstd2_ready")
        fin_ready = sem("fin_ready")
        out_stored = sem("out_stored")
        c_chain = sem("c_chain")
        mv_done = sem("mv_done")
        mv2_done = sem("mv2_done")
        xc_loaded = sem("xc_loaded")

        x_chunks = x.rearrange("b (h t p) d -> (b h) p t d", h=SEQ // CHUNK, p=P)
        out_chunks = out.rearrange("b (h t p) d -> (b h) p t d", h=SEQ // CHUNK, p=P)
        vaug = sb("vaug", [P, GROUPS, SEQ // P, GH, VW])
        ot = sb("ot", [P, HG, CHUNK])
        xc = sb("xc", [P, TPC, D])

        operands = ctx.enter_context(ExitStack())
        qs = operands.enter_context(nc.sbuf_tensor("qs", [P, 2, 2, PARTS, CHUNK], BF16))
        Qx, Kx, Qa, Ka = [operands.enter_context(nc.sbuf_tensor(name, [P, 2, GH, SEQ], BF16))
                          for name in ("Qx", "Kx", "Qa", "Ka")]

        def q_part(b, u, s):
            return q_scr[bass.ds(b * HG, HG), :, s, :, CHUNK * u:CHUNK * (u + 1)].rearrange("n h d t -> (n h) d t")

        def k_part(b, u, s):
            return k_scr[bass.ds(b * HG, HG), :, s, :, CHUNK * u:CHUNK * (u + 1)].rearrange("n h d t -> (n h) d t")

        def load_parts(eng, qdst, kdst, g, done):
            rows = PARTS * DH
            for r in range(PARTS):
                src = q_scr[g, :, r:r + PARTS, :, :].rearrange("n h s d t -> (n s d) h t")
                eng.dma_start(qdst[rows * r:rows * (r + 1), :, :], src).then_inc(done, 16)
                eng.dma_start(kdst[rows * r:rows * (r + 1), :, :],
                              k_scr[g].rearrange("n h s d t -> (n s d) h t")).then_inc(done, 16)

        STORES = 6

        def store_parts(sp, b):
            for u in range(2):
                sp.wait_ge(p2_made, 4 * b + 2 * u + 2)
                for s in (0, 1, 3, 4):
                    sp.dma_start(q_part(b, u, s), qs[:, u, 0, s % PARTS, :]).then_inc(qk_stored[u], 16)
                for s in (0, 1):
                    sp.dma_start(k_part(b, u, s), qs[:, u, 1, s, :]).then_inc(qk_stored[u], 16)

        with ExitStack() as phase:
            def sa(name, shape, dt=F32):
                return phase.enter_context(nc.sbuf_tensor(name, shape, dt))

            wqkv_nat = sa("wqkv_nat", [P, 3, P])
            wo_nat = sa("wo_nat", [P, P])
            down_nat = sa("down_nat", [P, FC, D])
            wq_nat = sa("wq_nat", [P, F])
            kbdT = sa("kbdT", [P, 4, P])
            WqT = sa("WqT", [P, 4, P])
            kbd = sa("kbd", [P, 4, P])
            xin = sa("xin", [P, 2, TPC, D])
            xT = sa("xT", [P, 2, CHUNK])
            qf = sa("qf", [P, 2, 2, CHUNK])
            rf = sa("rf", [P, 2, 2, CHUNK])

            with nc.Block() as block:
                @block.sync
                def _(sp):
                    for signal in (*qk_stored, v_ready, p3_made, s_ready, *o_stored, o_read, oT_ready, xb_ready, z_done,
                                   out_ready, h_ready, Wt_ready, sim_copied, attn_ready, out_stored,
                                   z2_done):
                        sp.sem_inc(signal, ONE)
                    sp.dma_start(down_nat[:], down.rearrange("(c p) d -> p c d", p=P)).then_inc(prep_loaded, 16)
                    sp.dma_start(wq_nat[:], Wq).then_inc(prep_loaded, 16)
                    sp.dma_start(wo_nat[:], W_o).then_inc(prep_loaded, 16)
                    sp.wait_ge(kbd_zeroed, 1)
                    for p in range(2):
                        for h in range(RH):
                            hl = h % 2
                            sp.dma_start(kbdT[64 * hl:64 * hl + 64, 2 * p + h // 2, 64 * hl:64 * hl + 64],
                                         keys[h, :, p, :]).then_inc(prep_loaded, 16)
                    sp.dma_start(Wg_sb[:], Wg).then_inc(wts_loaded, 16)
                    sp.dma_start(Wu_sb[:], Wu).then_inc(wts_loaded, 16)
                    sp.dma_start(Wd_sb[:], Wd.rearrange("(c p) d -> p c d", p=P)).then_inc(wts_loaded, 16)
                    sp.dma_start(up_sb[:], up.rearrange("(c p) d -> p c d", p=P)).then_inc(wts_loaded, 16)
                    for i, bias in enumerate((bg, bu)):
                        sp.dma_start(bgu[:, i, :], bias.rearrange("(c p) -> p c", p=P),
                                     allow_slow_non_contiguous=True).then_inc(wts_loaded, 16)
                    sp.dma_start(bo_row[:], b_o.rearrange("(o d) -> o d", o=1).broadcast_to([P, D])).then_inc(wts_loaded, 16)
                    sp.dma_start(bd_row[:], bd.rearrange("(o d) -> o d", o=1).broadcast_to([P, D])).then_inc(wts_loaded, 16)

                    with sp.Fori(0, BATCH - 1) as b:
                        store_parts(sp, b)
                    for u in range(2):
                        sp.wait_ge(qk_stored[u], STORES * 16 + ONE)
                        sp.wait_ge(p3_stored[u], 32)
                    sp.wait_ge(pads_made, 2)
                    load_parts(sp, Qx[:, 0], Kx[:, 0], bass.ds(0, 1), xop_loaded[0])
                    sp.wait_ge(wts_loaded, 16 * 8)

                @block.gpsimd
                def _(pool):
                    pool.memset(ident[:], 0.0).then_inc(consts_made, 1)
                    pool.wait_ge(consts_made, 1)
                    pool.affine_select(out=ident[:], in_=ident[:], compare_op=ALU.not_equal, fill=1.0, base=0,
                                       pattern=[[1, P]], channel_multiplier=-1).then_inc(consts_made, 1)
                    pool.memset(kbdT[:], 0.0).then_inc(kbd_zeroed, 1)
                    pool.memset(vaug[:], 1.0).then_inc(consts_made, 1)
                    pool.memset(mhalf[:], -0.5)
                    pool.iota(iota8[:], pattern=[[1, XIN]], base=0, channel_multiplier=0,
                              allow_small_or_imprecise_dtypes=True).then_inc(consts_made, 1)
                    pool.memset(Kx[:], 0.0).then_inc(pads_made, 1)

                    def third_parts(b, store=True):
                        for u in range(2):
                            if not isinstance(b, int) or b > 0:
                                pool.wait_ge(p3_stored[u], 32 * b)
                            for w in range(2):
                                pool.wait_ge(p2_made, 4 * b + 2 * u + w + 1)
                                pool.tensor_tensor(qs[:, u, w, 2, :], rf[:, u, w, :], qs[:, u, w, 1, :],
                                                   ALU.subtract).then_inc(p3_made, 1)
                            if not store:
                                continue
                            pool.wait_ge(p3_made, 4 * b + 2 * u + 2 + ONE)
                            pool.dma_start(q_part(b, u, 2), qs[:, u, 0, 2, :]).then_inc(p3_stored[u], 16)
                            pool.dma_start(k_part(b, u, 2), qs[:, u, 1, 2, :]).then_inc(p3_stored[u], 16)

                    third_parts(0)
                    with pool.Fori(1, BATCH - 1) as b:
                        third_parts(b)
                    third_parts(BATCH - 1, store=False)

                @block.scalar
                def _(act):
                    act.dma_start(wqkv_nat[:], W_qkv.rearrange("(c p) d -> p c d", p=P)).then_inc(wqkv_loaded, 16)
                    bqkv = b_qkv.rearrange("(w p) -> p w", w=3)
                    act.dma_start(bqk[:], bqkv[:, 0:2], allow_slow_non_contiguous=True).then_inc(wqkv_loaded, 16)
                    act.dma_start(bv_row[:], b_qkv.rearrange("(w d) -> w d", w=3)[2:3, :].broadcast_to([P, D])).then_inc(wqkv_loaded, 16)
                    for u in range(2):
                        act.dma_start(xin[:, u, :, :], x_chunks[u]).then_inc(x_loaded[u], 16)
                    def turned_weights(n, bank, dst):
                        act.wait_ge(wT_ready, n)
                        src = ps[:, bank, 0:dst.free_size()]
                        if len(dst.shape) == 3:
                            src = src.rearrange("p (a b) -> p a b", b=P)
                        act.activation(dst, src, ACT.Copy).then_inc(wT_read, 1)

                    turned_weights(1, 0, WqkvT[:, :, :])
                    act.wait_ge(wqkv_loaded, 48)
                    act.sem_inc(q_read, 2 * FREE)

                    def first_parts(b, more):
                        for u in range(2):
                            if more:
                                act.wait_ge(xT_ready, 2 * b + u + 1)
                                act.dma_start(xin[:, u, :, :], x_chunks[bass.ds(2 * b + u + 2, 1)].rearrange(
                                    "c p t d -> (c p) t d")).then_inc(x_loaded[u], 16)
                            act.wait_ge(qk_stored[u], STORES * 16 * b + ONE)
                            for w in range(2):
                                act.wait_ge(qk_ready, 4 * b + 2 * u + w + 1)
                                act.activation(qf[:, u, w, :], ps[:, 2 + 2 * w + u, :], ACT.Identity,
                                               bias=bqk[:, w:w + 1])
                                act.activation(qs[:, u, w, 0, :], ps[:, 2 + 2 * w + u, :], ACT.Identity,
                                               bias=bqk[:, w:w + 1]).then_inc(q_read, 1)

                    with act.Fori(0, BATCH - 1) as b:
                        first_parts(b, True)
                    first_parts(BATCH - 1, False)
                    for n, (bank, dst) in enumerate(((1, WoT[:, :]), (2, downT[:, :]), (3, WqT[:, :, :]),
                                                     (4, kbd[:, :, :]), (5, Wsim[:, :, :]))):
                        turned_weights(n + 2, bank, dst)

                @block.tensor
                def _(pe):
                    pe.wait_ge(consts_made, 2)
                    pe.wait_ge(wqkv_loaded, 48)
                    for w in range(3):
                        mm = pe.transpose(ps[:, 0, P * w:P * (w + 1)], wqkv_nat[:, w, :], ident[:])
                    mm.then_inc(wT_ready, 1)
                    pe.wait_ge(wT_read, 1)

                    def turn(b, u):
                        n = 2 * b + u
                        pe.wait_ge(x_loaded[u], 16 * b + 16)
                        pe.wait_ge(xT_read, n + 1)
                        for t in range(TPC):
                            mm = pe.transpose(ps[:, u, P * t:P * (t + 1)], xin[:, u, t, :], ident[:])
                        mm.then_inc(xT_ready, 1)

                    def project(b, u):
                        n = 2 * b + u
                        pe.wait_ge(xT_read, n + 1 + FREE)
                        for w in range(2):
                            pe.wait_ge(q_read, 2 * n + w + 1)
                            pe.matmul(ps[:, 2 + 2 * w + u, :], WqkvT[:, w, :], xT[:, u, :],
                                      start=True, stop=True).then_inc(qk_ready, 1)
                        pe.wait_ge(v_read, n + 1)
                        for t in range(TPC):
                            mm = pe.matmul(ps[:, 6 + u, P * t:P * (t + 1)], xT[:, u, P * t:P * (t + 1)],
                                           WqkvT[:, 2, :], start=True, stop=True)
                        mm.then_inc(v_ready, 1)

                    turn(0, 0)
                    with pe.Fori(0, BATCH - 1) as b:
                        turn(b, 1)
                        project(b, 0)
                        turn(b + 1, 0)
                        project(b, 1)
                    turn(BATCH - 1, 1)
                    project(BATCH - 1, 0)
                    project(BATCH - 1, 1)
                    pe.wait_ge(xT_read, 2 * BATCH + FREE)
                    pe.wait_ge(q_read, 4 * BATCH + 2 * FREE)
                    pe.wait_ge(prep_loaded, 16 * 11)
                    pe.transpose(ps[:, 1, 0:P], wo_nat[:], ident[:]).then_inc(wT_ready, 1)
                    for bank, blocks in ((2, [down_nat[:, c, :] for c in range(4)]),
                                         (3, [wq_nat[:, P * c:P * (c + 1)] for c in range(4)]),
                                         (4, [kbdT[:, c, :] for c in range(4)])):
                        for c in range(4):
                            mm = pe.transpose(ps[:, bank, P * c:P * (c + 1)], blocks[c], ident[:])
                        mm.then_inc(wT_ready, 1)
                    pe.wait_ge(wT_read, 5)
                    for c in range(4):
                        mm = pe.matmul(ps[:, 5, P * c:P * (c + 1)], WqT[:, c, :], kbd[:, c, :], start=True, stop=True)
                    mm.then_inc(wT_ready, 1)

                @block.vector
                def _(dve):
                    dve.sem_inc(xT_read, FREE)
                    dve.sem_inc(v_read, FREE)
                    dve.memset(Qx[:], 0.0).then_inc(pads_made, 1)
                    dve.wait_ge(consts_made, 3)
                    dve.wait_ge(wqkv_loaded, 48)

                    def copy_turned(b, u):
                        n = 2 * b + u
                        dve.wait_ge(xT_ready, n + 1)
                        if not isinstance(b, int) or b > 0:
                            dve.wait_ge(v_ready, n - 1 + ONE)
                        dve.tensor_copy(xT[:, u, :], ps[:, u, :]).then_inc(xT_read, 1)

                    def split(b, u):
                        n = 2 * b + u
                        for w in range(2):
                            dve.wait_ge(q_read, 2 * n + w + 1 + 2 * FREE)
                            dve.wait_ge(p3_made, 4 * b + ONE)
                            dve.tensor_tensor(rf[:, u, w, :], qf[:, u, w, :], qs[:, u, w, 0, :],
                                              ALU.subtract).then_inc(r_made, 1)
                            dve.wait_ge(r_made, 2 * n + w + 1)
                            dve.tensor_copy(qs[:, u, w, 1, :], rf[:, u, w, :]).then_inc(p2_made, 1)
                        dve.wait_ge(v_ready, n + 1 + ONE)
                        for t in range(TPC):
                            dst = vaug[:, bass.ds(b * HG, HG), TPC * u + t, :, 0:DH]
                            last = dve.tensor_tensor(dst, ps[:, 6 + u, P * t:P * (t + 1)].rearrange(
                                "p (g h d) -> p g h d", g=HG, d=DH), bv_row[:].rearrange(
                                "p (g h d) -> p g h d", g=HG, d=DH), ALU.add)
                        last.then_inc(v_read, 1)

                    copy_turned(0, 0)
                    copy_turned(0, 1)
                    with dve.Fori(0, BATCH - 1) as b:
                        for u in range(2):
                            split(b, u)
                            copy_turned(b + 1, u)
                    split(BATCH - 1, 0)
                    split(BATCH - 1, 1)

        with ExitStack() as phase:
            def sa(name, shape, dt=F32):
                return phase.enter_context(nc.sbuf_tensor(name, shape, dt))

            probs = sa("probs", [P, 2, GH, 2 * CHUNK])
            Vg = sa("Vg", [P, 2, SEQ // P, GH, VW])
            Os = sa("Os", [P, 2, CHUNK])
            tri = sa("tri", [P, CHUNK])
            junk = sa("junk", [P, 4, CHUNK], BF16)
            mx = sa("mx", [P, GH, SEQ // P, 2])
            mm_ = sa("rowmax", [P, 32])
            mr = sa("mr", [P, 32])
            msp = sa("msp", [P, PARTS * 32], BF16)
            mT = sa("mT", [P, PARTS * 32], BF16)

            with nc.Block() as block:
                @block.sync
                def _(sp):
                    def m_rows(g, u, reg):
                        sp.wait_ge(m_chain, M_STEPS * (g + 1))
                        sp.dma_start(m_scr[reg].rearrange("n p c -> (n p) c"), mT[:]).then_inc(m_stored, 16)
                        sp.wait_ge(m_stored, 16 * (g + 1))
                        src = m_scr[reg].rearrange("n (b c) (s r) -> b (n s) c r", b=4, s=PARTS)
                        for blk in range(4):
                            dst = Qa[M_ROW:M_ROW + PARTS, u, :, :].rearrange(
                                "s h (i b r) -> s b (h i) r", b=4, r=32)[:, blk]
                            sp.dma_start(dst, src[blk]).then_inc(mrow_loaded[u], 16)

                    load_parts(sp, Qx[:, 1], Kx[:, 1], bass.ds(1, 1), xop_loaded[1])
                    store_parts(sp, BATCH - 1)
                    for u in range(2):
                        sp.wait_ge(p3_made, 4 * (BATCH - 1) + 2 * u + 2 + ONE)
                        sp.dma_start(q_part(BATCH - 1, u, 2), qs[:, u, 0, 2, :]).then_inc(qk_stored[u], 16)
                        sp.dma_start(k_part(BATCH - 1, u, 2), qs[:, u, 1, 2, :]).then_inc(qk_stored[u], 16)
                    sp.wait_ge(pads_made, 5)
                    load_parts(sp, Qa[:, 0], Ka[:, 0], bass.ds(0, 1), sop_loaded[0])
                    for u in range(2):
                        sp.wait_ge(qk_stored[u], STORES * 16 * BATCH + 32 + ONE)
                        sp.wait_ge(p3_stored[u], 32 * (BATCH - 1))
                    m_rows(0, 0, bass.ds(0, 1))

                    def store_o(n, half):
                        sp.wait_ge(o_read, 2 * n + half + 1 + ONE)
                        sp.dma_start(o_scr[bass.ds(n, 1), :, CHUNK * half:CHUNK * (half + 1)].rearrange(
                            "n p t -> (n p) t"), Os[:, half, :]).then_inc(o_stored[half], 16)

                    def group(n, u, last):
                        if last < 1:
                            sp.wait_ge(mx_read, CPG * (n + 1))
                            load_parts(sp, Qx[:, u], Kx[:, u], bass.ds(n + 2, 1), xop_loaded[u])
                        if last < 2:
                            sp.wait_ge(s_ready, SPG * n + ONE)
                            load_parts(sp, Qa[:, 1 - u], Ka[:, 1 - u], bass.ds(n + 1, 1), sop_loaded[1 - u])
                        store_o(n, 0)
                        if last < 2:
                            m_rows(n + 1, 1 - u, bass.ds(n + 1, 1))
                        store_o(n, 1)

                    with sp.Fori(0, GROUPS // 2 - 1) as i:
                        for u in range(2):
                            group(2 * i + u, u, 0)
                    group(GROUPS - 2, 0, 1)
                    group(GROUPS - 1, 1, 2)
                    for half in range(2):
                        sp.wait_ge(o_stored[half], 16 * HG * (BATCH - 1) + ONE)
                    sp.dma_start(ot[:], o_scr[0:HG, :, 0:CHUNK].rearrange("g p t -> p g t")).then_inc(ot_loaded, 16)
                    sp.dma_start(xc[:], x_chunks[0]).then_inc(xc_loaded, 16)

                @block.gpsimd
                def _(pool):
                    pool.memset(tri[:], 0.0).then_inc(consts_made, 1)
                    pool.wait_ge(consts_made, 5)
                    pool.affine_select(out=tri[:, CHUNK - P:CHUNK], in_=tri[:, CHUNK - P:CHUNK], compare_op=ALU.is_ge,
                                       fill=-BIG, base=0, pattern=[[-1, P]], channel_multiplier=1).then_inc(pads_made, 1)
                    pool.memset(Qa[:], 0.0).then_inc(pads_made, 1)
                    pool.memset(Ka[:], 1.0).then_inc(pads_made, 1)

                    def group(n):
                        for r, k in enumerate(DIAG_UNITS):
                            step = UNITS[k][1][1][3]
                            for hh in range(GH):
                                wait_alone(pool, exp_done, SPG * n + GH * k + hh + 1 + FREE, pads_made)
                                diag = probs[:, k % 2, hh, 0:2 * step].rearrange("p (a c) -> p a c", a=2)[:, :, 0:P]
                                pool.affine_select(out=diag, in_=diag, compare_op=ALU.is_ge, fill=0.0, base=0,
                                                   pattern=[[0, 2], [1, P]], channel_multiplier=-1).then_inc(masked, 1)

                    with pool.Fori(0, GROUPS) as n:
                        group(n)

                @block.scalar
                def _(act):
                    act.sem_inc(exp_done, FREE)

                    def copy_out(n, half):
                        act.wait_ge(pv_done, PPG * n + (HALF_PIECES if half == 0 else PPG) + PV_START)
                        act.wait_ge(o_stored[half], 16 * n + ONE)
                        act.activation(Os[:, half, :], ps[:, O_BANK, :], ACT.Copy).then_inc(o_read, 1)

                    def group(n):
                        for e in range(SPG):
                            k, hh = divmod(e, GH)
                            width = UNITS[k][2]
                            if e == COPY_AT[0]:
                                copy_out(n, 0)
                            if e == COPY_AT[1] and not isinstance(n, int):
                                copy_out(n - 1, 1)
                            if hh == 0:
                                act.wait_ge(pv_done, PPG * n + 2 * (k - 1) + PV_START)
                            act.wait_ge(s_ready, SPG * n + e + 1 + ONE)
                            bank = S_BANK + 2 * (e % 2)
                            act.activation(probs[:, k % 2, hh, 0:width],
                                           ps[:, bank:bank + 2, :].rearrange("p a c -> p (a c)")[:, 0:width],
                                           ACT.Exp, scale=SM_SCALE).then_inc(exp_done, 1)

                    group(0)
                    with act.Fori(1, GROUPS) as n:
                        group(n)
                    copy_out(GROUPS - 1, 1)

                @block.tensor
                def _(pe):
                    pe.sem_inc(pv_done, PV_START)

                    def max_chunk(base, f, u, load):
                        i, part, hh, c0, c1 = MAXC[f]
                        if f == 0:
                            pe.wait_ge(xop_loaded[u], load)
                        if not (isinstance(base, int) and base + f < X_SLOTS):
                            pe.wait_ge(mx_read, base + f + 1 - X_SLOTS)
                        pe.matmul(ps[:, X_BANK + f % X_SLOTS, 0:c1 - c0], Qx[:, u, hh, P * i:P * (i + 1)],
                                  Kx[:, u, hh, c0:c1], start=True, stop=True).then_inc(mx_ready, 1)

                    def products(n, u, r):
                        k, place = PIECES[r]
                        half, tiles, width = UNITS[k]
                        if r == 0:
                            pe.wait_ge(o_read, 2 * n + ONE)
                            pe.wait_ge(v_staged, n + 3)
                        if r == HALF_PIECES:
                            pe.wait_ge(o_read, 2 * n + 1 + ONE)
                        if place == 0 and k in DIAG_UNITS:
                            pe.wait_ge(masked, MPG * n + GH * (DIAG_UNITS.index(k) + 1))
                        elif place == 0:
                            pe.wait_ge(exp_done, SPG * n + GH * (k + 1) + FREE)
                        j, q0, w, off = tiles[place]
                        for hh in range(GH):
                            mm = pe.matmul(ps[32 * hh:32 * hh + VW, O_BANK, q0 - CHUNK * half:q0 - CHUNK * half + w],
                                           Vg[:, u, j, hh, :], probs[:, k % 2, hh, off:off + w],
                                           start=(j == 0), stop=(j == 4 * half + 3), skip_group_check=True)
                        mm.then_inc(pv_done, 1)

                    def scores(n, u, e, load):
                        k, hh = divmod(e, GH)
                        if e == 0:
                            pe.wait_ge(sop_loaded[u], 6 * 16 * load)
                            pe.wait_ge(mrow_loaded[u], 4 * 16 * load)
                        pe.wait_ge(exp_done, SPG * n + e + 1)
                        for j, q0, w, off in UNITS[k][1]:
                            bank = S_BANK + 2 * (e % 2) + off // CHUNK
                            mm = pe.matmul(ps[:, bank, off % CHUNK:off % CHUNK + w], Ka[:, u, hh, P * j:P * (j + 1)],
                                           Qa[:, u, hh, q0:q0 + w], start=True, stop=True)
                        mm.then_inc(s_ready, 1)

                    for f in range(CPG):
                        max_chunk(0, f, 0, 6 * 16)
                    for f in range(AHEAD):
                        max_chunk(CPG, f, 1, 6 * 16)

                    def group(n, u, turn, last):
                        e = f = r = 0
                        for step in GROUP_ORDER:
                            if step == "s":
                                scores(n, u, e, turn + 1)
                                e += 1
                            elif step == "p":
                                if r >= CARRIED:
                                    products(n, u, r - CARRIED)
                                elif not isinstance(n, int) or n > 0:
                                    products(n - 1, 1 - u, PPG - CARRIED + r)
                                r += 1
                            else:
                                if f + AHEAD < CPG and last < 2:
                                    max_chunk(CPG * (n + 1), f + AHEAD, 1 - u, 0)
                                elif f + AHEAD >= CPG and last < 1:
                                    max_chunk(CPG * (n + 2), f + AHEAD - CPG, u, 6 * 16 * (turn + 2))
                                f += 1

                    group(0, 0, 0, 0)
                    group(1, 1, 0, 0)
                    with pe.Fori(0, GROUPS // 2 - 2) as i:
                        for u in range(2):
                            group(2 * i + 2 + u, u, i + 1, 0)
                    group(GROUPS - 2, 0, GROUPS // 2 - 1, 1)
                    group(GROUPS - 1, 1, GROUPS // 2 - 1, 2)
                    for r in range(PPG - CARRIED, PPG):
                        products(GROUPS - 1, 1, r)

                @block.vector
                def _(dve):
                    dve.memset(ps[:, O_BANK, :], 0.0).then_inc(v_staged, 1)
                    dve.memset(mx[:], -BIG).then_inc(v_staged, 1)
                    dve.tensor_copy(Vg[:, 0, :, :, :], vaug[:, 0, :, :, :]).then_inc(v_staged, 1)
                    dve.wait_ge(v_staged, 3)
                    dve.wait_ge(pads_made, 3)

                    def max_chunk(base, f):
                        i, part, hh, c0, c1 = MAXC[f]
                        w = c1 - c0
                        src = ps[:, X_BANK + f % X_SLOTS, 0:w]
                        if c1 == P * (i + 1):
                            wait_alone(dve, mx_ready, base + f + 1, pads_made)
                        else:
                            dve.wait_ge(mx_ready, base + f + 1)
                        if c1 == P * (i + 1):
                            dve.tensor_tensor_reduce(out=junk[:, f % 4, 0:w], in0=src, in1=tri[:, CHUNK - w:CHUNK], scale=1.0,
                                                     scalar=-BIG, op0=ALU.add, op1=ALU.max,
                                                     accum_out=mx[:, hh, i, 1:2]).then_inc(mx_read, 1)
                        else:
                            dve.tensor_reduce(mx[:, hh, i, 0:1], src, AX.X, ALU.max).then_inc(mx_read, 1)

                    def split_max(g):
                        c = M_STEPS * g
                        dve.wait_ge(mx_read, CPG * (g + 1))
                        dve.tensor_tensor(mm_[:].rearrange("p (h i) -> p h i", h=GH), mx[:, :, :, 0], mx[:, :, :, 1],
                                          ALU.max).then_inc(m_chain, 1)
                        dve.wait_ge(m_chain, c + 1)
                        dve.tensor_scalar(msp[:, 0:32], mm_[:], -1.0, None, ALU.mult).then_inc(m_chain, 1)
                        dve.wait_ge(m_chain, c + 2)
                        dve.scalar_tensor_tensor(out=mr[:], in0=mm_[:], scalar=-1.0, in1=msp[:, 0:32], op0=ALU.mult,
                                                 op1=ALU.subtract).then_inc(m_chain, 1)
                        dve.wait_ge(m_chain, c + 3)
                        dve.tensor_copy(msp[:, 32:64], mr[:]).then_inc(m_chain, 1)
                        dve.wait_ge(m_chain, c + 4)
                        dve.tensor_tensor(msp[:, 64:96], mr[:], msp[:, 32:64], ALU.subtract).then_inc(m_chain, 1)
                        dve.wait_ge(m_chain, c + 5)
                        dve.wait_ge(m_stored, 16 * g)
                        dve.transpose(mT[:], msp[:]).then_inc(m_chain, 1)

                    for f in range(CPG):
                        max_chunk(0, f)
                    split_max(0)
                    for f in range(AHEAD):
                        max_chunk(CPG, f)

                    def group(n, u, last):
                        for f in range(CPG):
                            if f == 12 and last < 2:
                                dve.wait_ge(pv_done, PPG * n + PV_START)
                                dve.tensor_copy(Vg[:, 1 - u, :, :, :], vaug[:, bass.ds(n + 1, 1), :, :, :].rearrange(
                                    "p n j h d -> p (n j) h d")).then_inc(v_staged, 1)
                            if f + AHEAD < CPG and last < 2:
                                max_chunk(CPG * (n + 1), f + AHEAD)
                            elif f + AHEAD >= CPG and last < 1:
                                max_chunk(CPG * (n + 2), f + AHEAD - CPG)
                            if f + AHEAD == CPG - 1 and last < 2:
                                split_max(n + 1)

                    with dve.Fori(0, GROUPS // 2 - 1) as i:
                        for u in range(2):
                            group(2 * i + u, u, 0)
                    group(GROUPS - 2, 0, 1)
                    group(GROUPS - 1, 1, 2)

        operands.close()

        with ExitStack() as phase:
            def sa(name, shape, dt=F32):
                return phase.enter_context(nc.sbuf_tensor(name, shape, dt))

            PRH = 2 * RH
            xb = sa("xb", [P, TPC, D])
            rden = sa("rden", [P, 2, HEADS])
            attn = sa("attn", [P, 2, D])
            attnT = sa("attnT", [P, 2, P])
            z = sa("z", [P, TPC, D])
            stats = sa("stats", [P, 2, TPC, 6])
            mv = sa("mv", [P, 2, TPC, 2])
            veps = sa("veps", [P, 2, TPC])
            rstd = sa("rstd", [P, 2, TPC])
            x1 = sa("x1", [P, TPC, D])
            x1b = sa("x1b", [P, TPC, D])
            x1T = sa("x1T", [P, CHUNK])
            gate = sa("gate", [P, FC, CHUNK])
            upv = sa("upv", [P, FC, CHUNK])
            h = sa("h", [P, FC, CHUNK])
            sG = sa("sG", [P, FC, CHUNK])
            sim = sa("sim", [P, TPC, 2 * RH * NK])
            V = sa("V", [P, 2, TPC * RH, KPH])
            ixu = sa("ixu", [P, TPC * RH, KPH], U32)
            ixf = sa("ixf", [P, TPC * RH * KPH])
            ymark = sa("ymark", [P, TPC * RH, NK])
            cand = sa("cand", [P, TPC * RH, KPH, KPH])
            cmark = sa("cmark", [P, TPC * RH, KPH, KPH])
            T = sa("T", [P, TPC * RH, KPH])
            shift_x = sa("shift_x", [P, TPC * RH, XIN])
            shift_y = sa("shift_y", [P, TPC * RH, NK])
            shift_c = sa("shift_c", [P, TPC * RH, NK])
            edge_ab = sa("edge_ab", [P, PRH, KPH, KPH])
            edge_a = sa("edge_a", [P, PRH * KPH])
            edge_ax = sa("edge_ax", [P, PRH * KPH, XIN])
            edge_x = sa("edge_x", [P, TPC * RH, XIN])
            picked = sa("picked", [P, PRH * KPH, KPH])
            sum_a = sa("sum_a", [P, PRH, KPH])
            den = sa("den", [P, PRH])
            rz = sa("rz", [P, PRH])
            far = sa("far", [P, PRH, KPH])
            rest = sa("rest", [P, TPC * RH])
            exn = sa("exn", [P, TPC * RH, XIN])
            eym = sa("eym", [P, TPC * RH, NK])
            A = sa("A", [P, 2, RH, XIN, NK])
            E = sa("E", [P, 2, RH, XIN, NK])
            Wt = sa("Wt", [P, 2, FC, P])
            z2 = sa("z2", [P, TPC, D])
            fin = sa("fin", [P, TPC, D])

            ATTN, ATTNT, Y, X1T, RING, SIM, AT, OUT = 0, 1, 2, 1, (3, 4), 5, 6, 7
            PE_ORDER = ["ffn4", "front0'", "AT0", "ffn5", "front1'", "front2'", "front3'", "front4'", "front5'",
                        "AT1", "x1T'", "sim0'", "out0", "sim1'", "sim2'", "ffn0'", "AT2", "out1", "sim3'", "ffn1'",
                        "ffn2'", "AT3", "out2", "ffn3'", "out3"]
            DVE_ORDER = ["front0'", "front1'", "dense1", "front2'", "wt0", "front3'", "front4'", "front5'", "x1'",
                         "dense2", "wt1", "z2_0", "r1_0'", "dense3", "wt2", "z2_1", "r2_0'", "r1_1'", "wt3", "z2_2",
                         "dense0'", "z2_3", "var2", "r2_1'", "fin"]
            POOL_ORDER = ["xb'", "h0", "spread2", "pow'", "h1", "spread3", "shift0'", "spread0'", "shift1'",
                          "spread1'", "pow2", "x1b'"]
            ACT_ORDER = ["turned1", "turned2", "turned3", "x1T", "sim0", "sim1", "sim2", "ffn0", "exps0", "ffn1",
                         "ffn2", "sim3", "ffn3", "exps1", "ffn4", "turned0'", "ffn5"]

            def run(order, table, c, more=True, only=False):
                for name in order:
                    later = name.endswith("'")
                    if (only and not later) or (later and not (more or only)):
                        continue
                    what = name.rstrip("'")
                    at = c if only or not later else c + 1
                    key = what.rstrip("0123456789") if what not in table else what
                    if key in table and what in table:
                        table[what](at)
                    else:
                        table[key](at, int(what[len(key):]))

            with nc.Block() as block:
                @block.sync
                def _(sp):
                    def load(b, u):
                        c = 2 * b + u
                        sp.wait_ge(oT_ready, TPC * c + ONE)
                        sp.dma_start(ot[:], o_scr[bass.ds(b * HG, HG), :, CHUNK * u:CHUNK * (u + 1)].rearrange(
                            "g p t -> p g t")).then_inc(ot_loaded, 16)
                        sp.wait_ge(xb_ready, c + ONE)
                        sp.dma_start(xc[:], x_chunks[bass.ds(c, 1)].rearrange(
                            "c p t d -> (c p) t d")).then_inc(xc_loaded, 16)

                    def store(c):
                        sp.wait_ge(fin_ready, c + 1)
                        sp.dma_start(out_chunks[bass.ds(c, 1)].rearrange("c p t d -> (c p) t d"),
                                     fin[:]).then_inc(out_stored, 16)

                    load(0, 1)
                    with sp.Fori(0, BATCH - 2) as b:
                        for u in range(2):
                            load(b + 1, u)
                            store(2 * b + u)
                    for half in range(2):
                        sp.wait_ge(o_stored[half], 16 * GROUPS + ONE)
                    for u in range(2):
                        load(BATCH - 1, u)
                        store(2 * (BATCH - 2) + u)
                    store(CHUNKS - 2)
                    store(CHUNKS - 1)
                    sp.wait_ge(out_stored, 16 * CHUNKS + ONE)

                @block.gpsimd
                def _(pool):
                    def residual(c):
                        pool.wait_ge(xc_loaded, 16 * c + 16)
                        pool.wait_ge(z_done, TPC * c + ONE)
                        pool.tensor_tensor(xb[:], xc[:], bo_row[:].unsqueeze(1).broadcast_to([P, TPC, D]),
                                           ALU.add).then_inc(xb_ready, 1)

                    def power(c):
                        pool.wait_ge(var_ready, c + 1)
                        pool.tensor_tensor(rstd[:, 0, :], veps[:, 0, :], mhalf[:], ALU.pow).then_inc(rstd_ready, 1)

                    def power2(c):
                        pool.wait_ge(var2_ready, c + 1)
                        pool.tensor_tensor(rstd[:, 1, :], veps[:, 1, :], mhalf[:], ALU.pow).then_inc(rstd2_ready, 1)

                    def residual2(c):
                        pool.wait_ge(x1_ready, c + 1)
                        pool.wait_ge(z2_done, TPC * c + ONE)
                        pool.tensor_tensor(x1b[:], x1[:], bd_row[:].unsqueeze(1).broadcast_to([P, TPC, D]),
                                           ALU.add).then_inc(x1b_ready, 1)

                    def below_max(c, p):
                        pool.wait_ge(cand_ready, 2 * c + p + 1)
                        heads = slice(PRH * p, PRH * (p + 1))
                        pool.tensor_tensor(shift_x[:, heads, :].rearrange("p (t h) x -> p t h x", t=2),
                                           sim[:, 2 * p:2 * p + 2, 0:RH * NK].rearrange("p t (h x) -> p t h x", h=RH)[:, :, :, 0:XIN],
                                           V[:, 0, heads, 0:1].rearrange("p (t h) o -> p t h o", t=2)
                                           .broadcast_to([P, 2, RH, XIN]), ALU.subtract)
                        pool.tensor_tensor(shift_y[:, heads, :].rearrange("p (t h) y -> p t h y", t=2),
                                           sim[:, 2 * p:2 * p + 2, RH * NK:].rearrange("p t (h y) -> p t h y", h=RH),
                                           V[:, 1, heads, 0:1].rearrange("p (t h) o -> p t h o", t=2)
                                           .broadcast_to([P, 2, RH, NK]), ALU.subtract)
                        pool.tensor_tensor(shift_c[:, heads, :], cand[:, heads].rearrange("p h a b -> p h (a b)"),
                                           T[:, heads, 0:1].broadcast_to([P, PRH, NK]), ALU.subtract).then_inc(shifted, 1)

                    def spread(c, t):
                        m, s = TPC * c + t, t % 2
                        if t % 2 == 0:
                            pool.wait_ge(edge_ready, 2 * c + t // 2 + 1)
                        pool.wait_ge(AT_ready, m + 1)
                        pool.tensor_tensor(A[:, s], sim[:, t, RH * NK:].rearrange("p (h o y) -> p h o y", h=RH, o=1)
                                           .broadcast_to([P, RH, XIN, NK]),
                                           edge_x[:, RH * t:RH * (t + 1)].unsqueeze(3).broadcast_to([P, RH, XIN, NK]), ALU.subtract)
                        pool.tensor_tensor(E[:, s], eym[:, RH * t:RH * (t + 1)].unsqueeze(2).broadcast_to([P, RH, XIN, NK]),
                                           exn[:, RH * t:RH * (t + 1)].unsqueeze(3).broadcast_to([P, RH, XIN, NK]),
                                           ALU.mult).then_inc(de_ready, 1)

                    def hidden(c, part):
                        for f in range(2 * part, 2 * part + 2):
                            pool.wait_ge(ffn_read, 3 * FC * c + 2 * f + 2 + FREE)
                            pool.wait_ge(out_ready, TPC * c + ONE)
                            pool.tensor_tensor(h[:, f, :], gate[:, f, :], upv[:, f, :], ALU.mult).then_inc(h_ready, 1)

                    pool.sem_inc(de_ready, TPC)
                    steps = {"xb": residual, "pow": power, "pow2": power2, "x1b": residual2, "shift": below_max,
                             "spread": spread, "h": hidden}
                    run(POOL_ORDER, steps, 0, only=True)
                    with pool.Fori(0, CHUNKS - 1) as c:
                        run(POOL_ORDER, steps, c)
                    run(POOL_ORDER, steps, CHUNKS - 1, more=False)

                @block.scalar
                def _(act):
                    act.sem_inc(ffn_read, FREE)

                    def turned(c, t):
                        act.wait_ge(attnT_ready, TPC * c + t + 1)
                        if t >= 2:
                            act.wait_ge(y_ready, TPC * c + t - 1)
                        act.activation(attnT[:, t % 2, :], ps[:, ATTNT, 0:P], ACT.Copy).then_inc(attnT_copied, 1)

                    def x1_turned(c):
                        act.wait_ge(x1T_ready, c + 1)
                        act.activation(x1T[:], ps[:, X1T, :], ACT.Copy).then_inc(x1T_copied, 1)

                    def copy_sim(c, t):
                        act.wait_ge(sim_ready, TPC * c + t + 1)
                        act.wait_ge(de_ready, TPC * c + t + 1)
                        act.activation(sim[:, t, :], ps[:, SIM, :], ACT.Copy).then_inc(sim_copied, 1)

                    def ffn(c, part):
                        for k in range(2 * part, 2 * part + 2):
                            act.wait_ge(ffn_ready, 3 * FC * c + k + 1)
                            src = ps[:, RING[k % 2], :]
                            if k < 2 * FC:
                                f = k // 2
                                act.wait_ge(h_ready, FC * c + ONE)
                                act.activation((gate if k % 2 == 0 else upv)[:, f, :], src,
                                               ACT.Silu if k % 2 == 0 else ACT.Identity,
                                               bias=bgu[:, k % 2, f:f + 1]).then_inc(ffn_read, 1)
                            else:
                                act.wait_ge(Wt_ready, TPC * c + ONE)
                                act.activation(sG[:, k - 2 * FC, :], src, ACT.Silu).then_inc(ffn_read, 1)

                    def exps(c, p):
                        act.wait_ge(shifted, 2 * c + p + 1)
                        heads = slice(PRH * p, PRH * (p + 1))
                        for part in (shift_x, shift_y, shift_c):
                            last = act.activation(part[:, heads, :], part[:, heads, :], ACT.Exp)
                        last.then_inc(exps_ready, 1)

                    steps = {"turned": turned, "x1T": x1_turned, "sim": copy_sim, "ffn": ffn, "exps": exps}
                    run(ACT_ORDER, steps, 0, only=True)
                    with act.Fori(0, CHUNKS - 1) as c:
                        run(ACT_ORDER, steps, c)
                    run(ACT_ORDER, steps, CHUNKS - 1, more=False)

                @block.tensor
                def _(pe):
                    def front(c, step):
                        if step == 0:
                            pe.wait_ge(ot_loaded, 16 * c + 16)
                        if step < TPC:
                            pe.wait_ge(attn_ready, TPC * c + step + ONE)
                            for g in range(HG):
                                mm = pe.transpose(ps[:, ATTN, P * g:P * (g + 1)], ot[:, g, P * step:P * (step + 1)], ident[:])
                            mm.then_inc(oT_ready, 1)
                        t = step - 1
                        if 0 <= t < TPC:
                            pe.wait_ge(attn_ready, TPC * c + t + 1 + ONE)
                            if t > 0:
                                pe.wait_ge(attnT_copied, TPC * c + t)
                            elif not isinstance(c, int):
                                pe.wait_ge(x1T_copied, c)
                            pe.transpose(ps[:, ATTNT, 0:P], attn[:, t % 2, :], ident[:]).then_inc(attnT_ready, 1)
                        t = step - 2
                        if 0 <= t < TPC:
                            pe.wait_ge(attnT_copied, TPC * c + t + 1)
                            pe.wait_ge(z_done, TPC * c + t + ONE)
                            pe.matmul(ps[:, Y, 0:P], attnT[:, t % 2, :], WoT[:],
                                      start=True, stop=True).then_inc(y_ready, 1)

                    def x1_turn(c):
                        pe.wait_ge(x1_ready, c + 1)
                        pe.wait_ge(attnT_copied, TPC * c + TPC)
                        for t in range(TPC):
                            mm = pe.transpose(ps[:, X1T, P * t:P * (t + 1)], x1[:, t, :], ident[:])
                        mm.then_inc(x1T_ready, 1)

                    def sims(c, t):
                        if t == 0:
                            pe.wait_ge(x1T_copied, c + 1)
                        pe.wait_ge(sim_copied, TPC * c + t + ONE)
                        pe.matmul(ps[:, SIM, :], x1T[:, P * t:P * (t + 1)],
                                  Wsim[:].rearrange("p a b -> p (a b)"), start=True, stop=True).then_inc(sim_ready, 1)

                    def ffn(c, part):
                        for k in range(2 * part, 2 * part + 2):
                            if k == 0:
                                pe.wait_ge(x1T_copied, c + 1)
                            pe.wait_ge(ffn_read, 3 * FC * c + k + 1)
                            if k < 2 * FC:
                                w = (Wg_sb if k % 2 == 0 else Wu_sb)[:, P * (k // 2):P * (k // 2 + 1)]
                            else:
                                w = downT[:, P * (k - 2 * FC):P * (k - 2 * FC + 1)]
                            pe.matmul(ps[:, RING[k % 2], :], w, x1T[:], start=True, stop=True).then_inc(ffn_ready, 1)

                    def combine(c, t):
                        m, s = TPC * c + t, t % 2
                        pe.wait_ge(A_ready, m + 1)
                        pe.wait_ge(Wt_ready, m + ONE)
                        Af = A[:, s].rearrange("p h x y -> p h (x y)")
                        for e in range(FC):
                            for hd in range(RH):
                                mm = pe.matmul(ps[:, AT, P * e:P * (e + 1)], Af[:, hd, P * e:P * (e + 1)], ident[:],
                                               start=(hd == 0), stop=(hd == RH - 1))
                        mm.then_inc(AT_ready, 1)

                    def output(c, t):
                        m, s = TPC * c + t, t % 2
                        dst = ps[:, OUT, 0:P]
                        pe.wait_ge(h_ready, FC * c + FC + ONE)
                        pe.wait_ge(z2_done, m + ONE)
                        for f in range(FC):
                            pe.matmul(dst, h[:, f, P * t:P * (t + 1)], Wd_sb[:, f, :], start=(f == 0), stop=False)
                        pe.wait_ge(Wt_ready, m + 1 + ONE)
                        for e in range(FC):
                            mm = pe.matmul(dst, Wt[:, s, e, :], up_sb[:, e, :], start=False, stop=(e == FC - 1))
                        mm.then_inc(out_ready, 1)

                    pe.sem_inc(AT_ready, FREE)
                    steps = {"front": front, "x1T": x1_turn, "sim": sims, "ffn": ffn, "AT": combine, "out": output}
                    run(PE_ORDER, steps, 0, only=True)
                    with pe.Fori(0, CHUNKS - 1) as c:
                        run(PE_ORDER, steps, c)
                    run(PE_ORDER, steps, CHUNKS - 1, more=False)

                @block.vector
                def _(dve):
                    linked = {"now": 0, "before": 0}

                    def link(ins, alone=False):
                        linked["now"] += 1
                        ins.then_inc(c_chain, 1)
                        value = linked["before"] + linked["now"]
                        if alone:
                            wait_alone(dve, c_chain, value, consts_made)
                        else:
                            dve.wait_ge(c_chain, value)

                    def r1(c, p):
                        tiles, heads = range(2 * p, 2 * p + 2), range(PRH * p, PRH * (p + 1))
                        these = slice(PRH * p, PRH * (p + 1))
                        for t in tiles:
                            wait_alone(dve, sim_copied, TPC * c + t + 1 + ONE, consts_made)
                            for g in range(2 * RH):
                                last = dve.max(V[:, g // RH, RH * t + g % RH, :], sim[:, t, NK * g:NK * (g + 1)])
                        link(last, alone=True)
                        for j in heads:
                            t, hd = divmod(j, RH)
                            dve.max_index(ixu[:, j, :], V[:, 0, j, :], sim[:, t, NK * hd:NK * (hd + 1)])
                            dve.match_replace(ymark[:, j, :], V[:, 1, j, :],
                                              sim[:, t, NK * (RH + hd):NK * (RH + hd + 1)], BIG)
                        link(dve.tensor_tensor(cand[:, these], V[:, 0, these, :].unsqueeze(3).broadcast_to([P, PRH, KPH, KPH]),
                                               V[:, 1, these, :].unsqueeze(2).broadcast_to([P, PRH, KPH, KPH]),
                                               ALU.add), alone=True)
                        for j in heads:
                            last = dve.max(T[:, j, :], cand[:, j].rearrange("p a b -> p (a b)"))
                        last.then_inc(cand_ready, 1)
                        wait_alone(dve, cand_ready, 2 * c + p + 1, consts_made)
                        for j in heads:
                            dve.match_replace(cmark[:, j].rearrange("p a b -> p (a b)"), T[:, j, :],
                                              cand[:, j].rearrange("p a b -> p (a b)"), BIG)
                        link(dve.tensor_copy(ixf[:, KPH * PRH * p:KPH * PRH * (p + 1)],
                                             ixu[:, these].rearrange("p h a -> p (h a)")), alone=True)

                    def r2(c, p):
                        these = slice(PRH * p, PRH * (p + 1))
                        ix = ixf[:, KPH * PRH * p:KPH * PRH * (p + 1)]
                        dve.tensor_scalar(edge_ab[:], cmark[:, these], MARKED, FAR, ALU.is_lt, ALU.mult)
                        link(dve.tensor_tensor(edge_ax[:], ix.unsqueeze(2).broadcast_to([P, PRH * KPH, XIN]),
                                               iota8[:].unsqueeze(1).broadcast_to([P, PRH * KPH, XIN]),
                                               ALU.not_equal))
                        link(dve.tensor_tensor(edge_ab[:], edge_ab[:],
                                               V[:, 1, these, :].unsqueeze(2).broadcast_to([P, PRH, KPH, KPH]),
                                               ALU.add))
                        dve.tensor_reduce(edge_a[:], edge_ab[:].rearrange("p h a b -> p (h a) b"), AX.X, ALU.min)
                        dve.wait_ge(exps_ready, 2 * c + p + 1)
                        link(dve.scalar_tensor_tensor(out=picked[:], in0=cmark[:, these].rearrange("p h a b -> p (h a) b"),
                                                      scalar=MARKED,
                                                      in1=shift_c[:, these, :].rearrange("p h (a b) -> p (h a) b", b=KPH),
                                                      op0=ALU.is_ge, op1=ALU.mult))
                        dve.tensor_reduce(sum_a[:].rearrange("p h a -> p (h a)"), picked[:], AX.X, ALU.add)
                        link(dve.scalar_tensor_tensor(out=edge_ax[:], in0=edge_ax[:], scalar=FAR,
                                                      in1=edge_a[:].unsqueeze(2).broadcast_to([P, PRH * KPH, XIN]),
                                                      op0=ALU.mult, op1=ALU.add))
                        dve.tensor_reduce(den[:], sum_a[:], AX.X, ALU.add)
                        link(dve.scalar_tensor_tensor(out=far[:].rearrange("p h a -> p (h a)"), in0=ix,
                                                      scalar=float(XIN), in1=sum_a[:].rearrange("p h a -> p (h a)"),
                                                      op0=ALU.is_ge, op1=ALU.mult))
                        dve.reciprocal(rz[:], den[:])
                        dve.tensor_reduce(rest[:, these], far[:], AX.X, ALU.add)
                        link(dve.tensor_reduce(edge_x[:, these, :], edge_ax[:].rearrange("p (h a) x -> p h x a", h=PRH), AX.X,
                                               ALU.min))
                        dve.tensor_tensor(rest[:, these], rest[:, these], rz[:], ALU.mult)
                        dve.tensor_tensor(exn[:, these, :], shift_x[:, these, :],
                                          rz[:].unsqueeze(2).broadcast_to([P, PRH, XIN]), ALU.mult)
                        dve.scalar_tensor_tensor(out=eym[:, these, :], in0=ymark[:, these, :], scalar=MARKED,
                                                 in1=shift_y[:, these, :], op0=ALU.is_ge, op1=ALU.mult).then_inc(edge_ready, 1)

                    def dense(c, t):
                        m, s = TPC * c + t, t % 2
                        dve.wait_ge(de_ready, m + 1 + TPC)
                        flat = A[:, s].rearrange("p h x y -> p (h x y)")
                        link(dve.scalar_tensor_tensor(out=flat, in0=flat, scalar=0.0,
                                                      in1=E[:, s].rearrange("p h x y -> p (h x y)"),
                                                      op0=ALU.is_ge, op1=ALU.mult))
                        end = A[:, s, :, XIN - 1, NK - 1]
                        dve.tensor_tensor(end, end, rest[:, RH * t:RH * (t + 1)], ALU.add).then_inc(A_ready, 1)

                    def wt(c, t):
                        m, s = TPC * c + t, t % 2
                        dve.wait_ge(AT_ready, m + 1 + FREE)
                        if t == 0:
                            dve.wait_ge(ffn_read, 3 * FC * (c + 1) + FREE)
                        if t >= 2:
                            dve.wait_ge(out_ready, m - 1 + ONE)
                        dve.tensor_tensor(Wt[:, s], ps[:, AT, :].rearrange("p (e t) -> p e t", e=FC),
                                          sG[:, :, P * t:P * (t + 1)], ALU.mult).then_inc(Wt_ready, 1)

                    def moments(which, src, t, done):
                        link(dve.bn_stats(stats[:, which, t, :], src[:, t, :]), alone=True)
                        dve.bn_aggr(mv[:, which, t, :], stats[:, which, t, :]).then_inc(done, 1)

                    def front(c, step):
                        if step < TPC:
                            s = step % 2
                            dve.wait_ge(oT_ready, TPC * c + step + 1 + ONE)
                            src = ps[:, ATTN, :].rearrange("p (h r) -> p h r", r=32)
                            link(dve.reciprocal(rden[:, s, :], src[:, :, DH]))
                            dve.tensor_tensor(attn[:, s, :].rearrange("p (h d) -> p h d", d=DH), src[:, :, 0:DH],
                                              rden[:, s, :].unsqueeze(2).broadcast_to([P, HEADS, DH]),
                                              ALU.mult).then_inc(attn_ready, 1)
                        t = step - 2
                        if 0 <= t < TPC:
                            dve.wait_ge(y_ready, TPC * c + t + 1)
                            dve.wait_ge(xb_ready, c + 1 + ONE)
                            dve.tensor_tensor(z[:, t, :], ps[:, Y, 0:P], xb[:, t, :], ALU.add).then_inc(z_done, 1)
                            dve.wait_ge(z_done, TPC * c + t + 1 + ONE)
                            moments(0, z, t, mv_done)
                        if step == TPC + 1:
                            dve.wait_ge(mv_done, TPC * c + TPC)
                            dve.tensor_scalar(veps[:, 0, :], mv[:, 0, :, 1], EPS, None, ALU.add).then_inc(var_ready, 1)

                    def normalise(c):
                        dve.wait_ge(rstd_ready, c + 1)
                        if not isinstance(c, int):
                            dve.wait_ge(x1T_ready, c)
                            dve.wait_ge(x1b_ready, c)
                        for t in range(TPC):
                            last = dve.tensor_scalar(x1[:, t, :], z[:, t, :], mv[:, 0, t, 0:1], rstd[:, 0, t:t + 1],
                                                     ALU.subtract, ALU.mult)
                        last.then_inc(x1_ready, 1)

                    def last_sum(c, t):
                        m = TPC * c + t
                        dve.wait_ge(out_ready, m + 1 + ONE)
                        dve.wait_ge(x1b_ready, c + 1)
                        dve.tensor_tensor(z2[:, t, :], ps[:, OUT, 0:P], x1b[:, t, :], ALU.add).then_inc(z2_done, 1)
                        dve.wait_ge(z2_done, m + 1 + ONE)
                        moments(1, z2, t, mv2_done)

                    def variances(c):
                        dve.wait_ge(mv2_done, TPC * (c + 1))
                        dve.tensor_scalar(veps[:, 1, :], mv[:, 1, :, 1], EPS, None, ALU.add).then_inc(var2_ready, 1)

                    def finish(c):
                        dve.wait_ge(rstd2_ready, c + 1)
                        dve.wait_ge(out_stored, 16 * c + ONE)
                        for t in range(TPC):
                            last = dve.tensor_scalar(fin[:, t, :], z2[:, t, :], mv[:, 1, t, 0:1], rstd[:, 1, t:t + 1],
                                                     ALU.subtract, ALU.mult)
                        last.then_inc(fin_ready, 1)

                    steps = {"front": front, "x1": normalise, "r1_": r1, "r2_": r2, "dense": dense, "wt": wt,
                             "z2_": last_sum, "var2": variances, "fin": finish}
                    run(DVE_ORDER, steps, 0, only=True)
                    first = linked["now"]
                    with dve.Fori(0, CHUNKS - 1) as c:
                        linked.update(now=0, before=first + LINKS * c)
                        run(DVE_ORDER, steps, c)
                        assert linked["now"] == LINKS, linked["now"]
                    linked.update(now=0, before=first + LINKS * (CHUNKS - 1))
                    run(DVE_ORDER, steps, CHUNKS - 1, more=False)


_INS = ["L0_attn_x", "L0_attn_W_qkv", "L0_attn_b_qkv", "L0_attn_W_o", "L0_attn_b_o", "L0_ffn_Wg", "L0_ffn_bg",
        "L0_ffn_Wu", "L0_ffn_bu", "L0_ffn_Wd", "L0_ffn_bd", "L0_ffn_Wq", "L0_ffn_keys", "L0_ffn_down_embed",
        "L0_ffn_up_embed"]
_OUTS = [((4, 1024, 128), "float32")]


def kernel(**inputs):
    import numpy as _np
    import concourse.bacc as _bacc
    from concourse import mybir as _mybir
    from concourse.bass_utils import run_bass_kernel_spmd as _run

    nc = _bacc.Bacc("TRN2", target_bir_lowering=False, num_devices=1)
    arrays, args = {}, []
    for name in _INS:
        a = _np.ascontiguousarray(inputs[name])
        arrays[f"in_{name}_dram"] = a
        args.append(nc.dram_tensor(f"in_{name}_dram", a.shape, _mybir.dt.from_np(a.dtype), kind="ExternalInput").ap())
    for i, (shape, dtype) in enumerate(_OUTS):
        dt = _mybir.dt.from_np(_np.dtype(dtype))
        args.append(nc.dram_tensor(f"out_{i}_dram", shape, dt, kind="ExternalOutput").ap())
    build(nc, *args)
    r = _run(nc, [arrays], core_ids=[0])
    got = tuple(r.results[0][f"out_{i}_dram"] for i in range(len(_OUTS)))
    return got[0]
```
